# Optimizing a Trainium2 kernel written in Bass

```python
import numpy as np
import jax
import jax.numpy as jnp

def _softmax(x, axis=-1):
    return jax.nn.softmax(x, axis=axis)

def _gelu(x):
    return jax.nn.gelu(x, approximate=True)

def _silu(x):
    return jax.nn.silu(x)

def _sigmoid(x):
    return jax.nn.sigmoid(x)

def _layernorm(x, axis=-1, eps=1e-05):
    m = jnp.mean(x, axis=axis, keepdims=True)
    v = jnp.var(x, axis=axis, keepdims=True)
    return (x - m) / jnp.sqrt(v + eps)

def _scatter_add(tgt, idx, src, axis=0):
    return tgt.at[idx].add(src)

def _segment_sum(src, seg, n):
    return jax.ops.segment_sum(src, seg, n)
kernel_name = 'mk_gnn_preln_d1_gnn_r64_f49d95'

def setup_inputs(seed: int=0):
    np.random.seed(seed)
    _w = jnp.asarray

    def _rec_inputs():
        import jax
        import jax.numpy as jnp
        _gk = jax.random.key(seed)
        x = -0.0003713 + 1 * jax.random.normal(jax.random.fold_in(_gk, 1), (50000, 256), jnp.float32)
        src = jax.random.randint(jax.random.fold_in(_gk, 2), (12500,), 0, 50000, jnp.int32)
        dst = jnp.minimum((50000 * jax.random.uniform(jax.random.fold_in(_gk, 3), (12500,)) ** 2.0).astype(jnp.int32), 49999)
        _o = jnp.argsort(dst, stable=True)
        src = src[_o]
        dst = dst[_o]
        edge_type_8 = jax.random.randint(jax.random.fold_in(_gk, 12), (12500,), 0, 8, jnp.int32)
        return (x, src, dst, edge_type_8)
    x, src, dst, edge_type_8 = _rec_inputs()

    def _L0_gnn_setup():
        import jax, jax.numpy as jnp
        import numpy as np
        N_NODES = 50000
        N_EDGES = 12500
        D_IN = 256
        D_OUT = 256
        N_REL = 8
        key = jax.random.key(seed)
        k_x, k_ei, k_et, k_w = jax.random.split(key, 4)
        x = jax.random.normal(k_x, (N_NODES, D_IN), dtype=jnp.float32)
        edge_index = jax.random.randint(k_ei, (2, N_EDGES), 0, N_NODES, dtype=jnp.int32)
        edge_type = jax.random.randint(k_et, (N_EDGES,), 0, N_REL, dtype=jnp.int32)
        limit = float(np.sqrt(6.0 / (D_IN + D_OUT)))
        weight = jax.random.uniform(k_w, (N_REL, D_IN, D_OUT), dtype=jnp.float32, minval=-limit, maxval=limit)
        bias = jnp.zeros((D_OUT,), dtype=jnp.float32)
        return {'x': x, 'edge_index': edge_index, 'edge_type': edge_type, 'weight': weight, 'bias': bias}
    _L0_gnn_all = _L0_gnn_setup()
    _L0_gnn_in = {k: v for k, v in _L0_gnn_all.items() if k in ('weight', 'bias')}
    del _L0_gnn_all
    return {'x': x, 'src': src, 'dst': dst, 'edge_type_8': edge_type_8, 'L0_gnn_weight': _L0_gnn_in['weight'], 'L0_gnn_bias': _L0_gnn_in['bias']}

def reference(x, src, dst, edge_type_8, L0_gnn_weight, L0_gnn_bias):
    import jax
    import jax.numpy as jnp

    def _L0_gnn_ref(x, edge_index, edge_type, weight, bias):
        import jax, jax.numpy as jnp
        import numpy as np
        N_NODES = 50000
        N_EDGES = 12500
        D_IN = 256
        D_OUT = 256
        N_REL = 8
        num_nodes = x.shape[0]
        row, col = (edge_index[0], edge_index[1])
        xt = jnp.einsum('ni,rio->rno', x, weight)
        messages = xt[edge_type, col]
        out = jax.ops.segment_sum(messages, row, num_segments=num_nodes)
        return jax.nn.relu(out + bias)
    edge_index = jnp.stack([src, dst])
    h = jnp.maximum(_layernorm(x, axis=-1), 0.0)
    x = x + _L0_gnn_ref(h, edge_index, edge_type_8, L0_gnn_weight, L0_gnn_bias)
    return x

_drawn_inputs = setup_inputs


def setup_inputs(seed=0):
    import zlib

    import numpy as np

    out = dict(_drawn_inputs(seed))
    spreads = {'L0_gnn_bias': (0.0, 0.1)}
    factors = {}
    for name, (base, spread) in spreads.items():
        noise = np.random.default_rng([zlib.crc32(name.encode()), seed]).standard_normal(out[name].shape)
        drawn = base * np.exp(spread * noise) if base else spread * noise
        out[name] = jnp.asarray(drawn.astype(out[name].dtype))
    for name, factor in factors.items():
        out[name] = (out[name] * factor).astype(out[name].dtype)
    return out
```

```python
from contextlib import ExitStack

import concourse.bass as bass
from concourse import mybir
from concourse.alu_op_type import AluOpType as ALU

P = 128
ACT = mybir.ActivationFunctionType
AX_X = mybir.AxisListType.X
F32 = mybir.dt.float32
F16 = mybir.dt.float16
BF16 = mybir.dt.bfloat16
I32 = mybir.dt.int32
EPS = 1e-5


class Count:

    def __init__(self, eng, sem):
        self.eng, self.sem, self.base, self.n, self.per, self.saved = eng, sem, 0, 0, 0, 0

    def up(self, ins):
        ins.then_inc(self.sem, 1)
        self.n += 1
        return self.base + self.n

    def wait(self, value):
        self.eng.wait_ge(self.sem, value)

    def chain(self, ins):
        self.wait(self.up(ins))

    def loop(self, i, per):
        self.saved, self.per = self.n, per
        self.base, self.n = i * per + self.n, 0

    def end(self, trips):
        assert self.n == self.per, (self.n, self.per)
        self.base, self.n = 0, self.saved + trips * self.per


def gnn_kernel(nc, x, src, dst, edge_type, weight, bias, out):
    NODES, D = x.shape
    E = src.shape[0]
    R = weight.shape[0]
    KC = D // P
    EP = max(p for p in range(1, P + 1) if E % p == 0)
    EC = E // EP
    MT = (E - R) // P + R
    LANES = 5
    RING = 3
    NG = MT // LANES
    LAPS = NG // RING
    ECP = NG * LANES
    TB = LANES * RING
    assert MT == NG * LANES and NG == LAPS * RING and EC <= ECP and EP <= P
    BL = 3
    WIN = BL * P
    NW = -(-NODES // WIN)
    GW = 2
    XK = 5
    WB = GW * XK
    XLAPS = (NW - 1) // WB
    XRING = 2
    TAIL = NODES - (NW - 1) * WIN
    TAILP = -(-TAIL // BL)
    TAILF = TAIL // BL
    assert NW - 1 == XLAPS * WB and 0 < TAIL < WIN and XLAPS > XRING
    assert TAILP > TAILF
    ROWS = MT * P
    NONE = 1 << 17
    assert ROWS // 8 + 16 <= 2048 and WIN <= 512 and NODES < 1 << 16
    RB = 8
    assert R <= RB
    DIV = 171
    assert BL == 3 and NODES >> 7 < 512
    L0 = 3 * NW
    L1 = (LANES - 3) * NW

    msg = nc.dram_tensor("messages", (ROWS, D), F32, kind="Internal").ap()
    msg_by_lane = msg.rearrange("(p t) d -> p t d", t=MT)

    with ExitStack() as ctx:
        def sb(name, shape, dt):
            return ctx.enter_context(nc.sbuf_tensor(name, shape, dt))

        def sem(name):
            return ctx.enter_context(nc.semaphore(name))

        iota_n = max(P, MT, NW)
        iota16 = sb("iota16", [P, iota_n], F16)
        iota_node = sb("iota_node", [P, BL, P], F32)
        part = sb("part", [P, 1], F32)
        ident = sb("ident", [P, P], F32)
        ident16 = sb("ident16", [P, P], F16)
        before16 = sb("before16", [P, P], F16)
        ones16 = sb("ones16", [P, P], F16)
        eps = sb("eps", [P, 1], F32)
        zeros16 = sb("zeros16", [P, P], F16)
        ones_b = sb("ones_b", [3, P], BF16)
        bias_part = sb("bias_part", [3, 3, D], BF16)
        bias_sel = sb("bias_sel", [3, 2, D], BF16)
        bias3 = sb("bias3", [3, 2, D], BF16)
        W = sb("W", [P, R * KC * D], F32)

        typ_i = sb("typ_i", [EP, EC], I32)
        dst_i = sb("dst_i", [EP, EC], I32)
        src_i = sb("src_i", [EP, EC], I32)
        typ16 = sb("typ16", [EP, EC], F16)
        tmp_i = sb("tmp_i", [EP, 8, EC], I32)
        pos = sb("pos", [EP, EC], F32)
        pos_i = sb("pos_i", [EP, EC], I32)
        srel = sb("srel", [EP, EC], F32)
        v2f = sb("v2f", [EP, EC], F32)
        cols = sb("cols", [EP, 7, ECP], F16)
        lane16, tile16, win16, dhi16, dlo16, v1, v2 = (cols[:, k, :] for k in range(7))
        rank16 = sb("rank16", [EP, ECP], F16)
        over = sb("over", [EP, ECP], F16)
        over_n = sb("over_n", [EP, 1], F32)
        over16 = sb("over16", [EP, 1], F16)
        over_i = sb("over_i", [P, 1], I32)
        base = sb("base", [EP, R], F32)
        cnt_i = sb("cnt_i", [P, 2, R], I32)
        tiles = sb("tiles", [P, 2, 2 * R], F32)
        rel_ge = sb("rel_ge", [1, MT, R], F32)
        rel_f = sb("rel_f", [1, MT], F32)
        rel_p = sb("rel_p", [1, LANES, NG], F32)
        rel_i = sb("rel_i", [1, NG], I32)
        dlo_f = sb("dlo_f", [P, MT], F32)
        dst_list = sb("dst_list", [P, MT], I32)
        OHW = sb("OHW", [EP, ECP, NW], F16)
        LT = sb("LT", [EP, LANES, NW], F16)
        C = sb("C", [EP, LANES, NW], F16)
        prod = sb("prod", [EP, LANES, NW], F16)
        OHR = sb("OHR", [EP, RING, LANES, P], F16)
        RV = sb("RV", [EP, RING, LANES, 2, P], F16)

        row_list = sb("row_list", [P, NW], I32)
        src_list = sb("src_list", [P, NW], F32)

        xg = sb("xg", [P, TB, D], F32)
        mg = sb("mg", [P, TB, D], F32)
        hT = sb("hT", [P, RING, KC * P], F32)
        stage1 = sb("stage1", [P, RING, LANES], I32)
        stats = sb("stats", [P, RING, LANES, 6], F32)
        mv = sb("mv", [P, RING, LANES, 2], F32)
        std = sb("std", [P, RING, LANES], F32)
        rstd = sb("rstd", [P, RING, LANES], F32)
        nmr = sb("nmr", [P, RING, LANES], F32)

        SCR = WB * D + 5 * WIN
        scratch = sb("scratch", [P, SCR], F32)
        gm = scratch[:, 0:WB * D].rearrange("p (w d) -> p w d", d=D)
        S = scratch[:, WB * D:SCR].rearrange("p (s b n) -> p s b n", s=5, b=BL)
        PADC = 64
        scan_w = R * (PADC + EC) // 2
        scan = [scratch[0:EP, k * scan_w:(k + 1) * scan_w].bitcast(F16).rearrange("p (r c) -> p r c", r=R)
                for k in range(3)]
        sc_sum, sc_sel = (mg[0:EP, :, :].rearrange("p t d -> p (t d)")[:, k * R * EC:(k + 1) * R * EC]
                          .rearrange("p (r c) -> p r c", r=R) for k in range(2))
        bias_row = hT[0:3, 0, 0:D]
        bias_rest = hT[0:3, 1:3, 0:D]
        li_f = scratch[:, WB * D:WB * D + 10 * NW].rearrange("p (k w) -> p k w", w=NW)
        li = li_f[:, 0:6, :].bitcast(I32)
        lv, row_f, empty = li_f[:, 6, :], li_f[:, 7:9, :], li_f[:, 9, :]
        assert 10 * NW <= 5 * WIN
        at = 0
        OHL, OHT, HV = [], [], []
        for g in range(RING):
            for lst, n in ((OHL, P), (OHT, MT + 1), (HV, 2 * MT)):
                w = LANES * n // 2
                v = scratch[0:EP, at:at + w].bitcast(F16).rearrange("p (c n) -> p c n", c=LANES)
                lst.append(v)
                at += w
        assert at <= SCR and 3 * scan_w <= SCR
        stage3 = sb("stage3", [P, 2, WB // 2], I32)
        XS = XRING * XK
        xr = sb("xr", [P, XS * GW, BL * D], F32)
        xt = sb("xt", [TAILP, BL * D], F32)

        a_val, a_pos = (mg[0:EP, k, 0:2 * EC].rearrange("p (k c) -> p k c", k=2) for k in range(2))
        a_lane = RV[:, 0, 0, 0, :]
        a_tile = OHW[:, 0:2, :].rearrange("p c w -> p (c w)")[:, 0:2 * MT]
        src_slot = mg[:, 2, 0:MT]

        ps = ctx.enter_context(nc.psum_tensor("ps", [P, 8 * 512], F32))

        def bank(b, a, z, parts=P):
            return ps[0:parts, 512 * b + a:512 * b + z]

        ps_T = [bank(b, 0, KC * P) for b in (0, 1, 4)]
        ps_M = [bank(b, 0, D) for b in (2, 3, 5)]
        ps_L0, ps_L1 = bank(4, 0, L0, EP), bank(5, 0, L1, EP)
        ps_dst = bank(6, 0, 2 * MT)
        ps_over = bank(6, 0, 1)
        ps_rel = bank(7, 0, R, EP)
        ps_cnt = bank(7, R, 2 * R)
        ps_win = bank(7, 0, 2 * NW)
        ps_W = [ps[:, 1024 * k:1024 * k + BL * D] for k in range(2)]
        assert L0 <= 512 and 2 * MT <= 512 and BL * D <= 1024

        s_edge = sem("s_edge")
        s_bias = sem("s_bias")
        s_w = sem("s_w")
        s_tail = sem("s_tail")
        s_iota = sem("s_iota")
        s_dve = sem("s_dve")
        s_const = sem("s_const")
        s_tot = sem("s_tot")
        s_relps = sem("s_relps")
        s_sc = sem("s_sc")
        s_scps = sem("s_scps")
        s_dstps = sem("s_dstps")
        s_list = sem("s_list")
        s_ohw = sem("s_ohw")
        s_lt = sem("s_lt")
        s_stage = sem("s_stage")
        s_gather = [sem(f"s_gather{g}") for g in range(RING)]
        s_var = sem("s_var")
        s_std = sem("s_std")
        s_ln = sem("s_ln")
        s_norm = sem("s_norm")
        s_T = sem("s_T")
        s_hT = sem("s_hT")
        s_mm = sem("s_mm")
        s_mg = sem("s_mg")
        s_mst = [sem(f"s_mst{g}") for g in range(RING)]
        s_rv = sem("s_rv")
        s_rvps = sem("s_rvps")
        s_held = sem("s_held")
        s_zero = sem("s_zero")
        s_win = sem("s_win")
        s_overps = sem("s_overps")
        s_over = sem("s_over")
        s_wg = [sem(f"s_wg{k}") for k in range(WB)]
        s_sel = sem("s_sel")
        s_wmm = sem("s_wmm")
        s_fin = sem("s_fin")
        s_x = [sem(f"s_x{k}") for k in range(XK)]
        s_out = [sem(f"s_out{k}") for k in range(XK)]
        s_outt = sem("s_outt")
        s_a_sc = sem("s_a_sc")
        s_a_ps = sem("s_a_ps")
        s_a_list = sem("s_a_list")
        s_a_msg = sem("s_a_msg")
        s_a_sel = sem("s_a_sel")
        s_a_mm = sem("s_a_mm")
        s_a_win = sem("s_a_win")
        s_a_x = sem("s_a_x")
        s_a_out = sem("s_a_out")

        x_groups = x[0:XLAPS * WB * WIN, :].rearrange("(g w p b) d -> g p w (b d)", w=GW, p=P, b=BL)
        out_groups = out[0:XLAPS * WB * WIN, :].rearrange("(g w p b) d -> g p w (b d)", w=GW, p=P, b=BL)
        x_wins = x[0:XLAPS * WB * WIN, :].rearrange("(w p b) d -> w p (b d)", p=P, b=BL)
        out_wins = out[0:XLAPS * WB * WIN, :].rearrange("(w p b) d -> w p (b d)", p=P, b=BL)
        t0 = (NW - 1) * WIN
        tail_full = slice(t0, t0 + TAILF * BL)
        tail_rest = slice(t0 + TAILF * BL, NODES)
        REST = NODES - tail_rest.start

        def tail_dma(eng, dram, tile, load, done):
            full = dram[tail_full, :].rearrange("(p b) d -> p (b d)", b=BL)
            rest = dram[tail_rest, :].rearrange("(p b) d -> p (b d)", b=REST)
            for d, s in ((full, tile[0:TAILF, :]), (rest, tile[TAILF:TAILP, 0:REST * D])):
                eng.dma_start(*((s, d) if load else (d, s))).then_inc(done, 16)

        def x_slot(lap, k):
            return (lap % XRING) * WB + k * GW

        block = ctx.enter_context(nc.Block())

        @block.sync
        def _(sp):
            for t, d in ((typ_i, edge_type), (dst_i, dst), (src_i, src)):
                sp.dma_start(t[:, :], d.rearrange("(p c) -> p c", c=EC)).then_inc(s_edge, 16)
            for k in range(3):
                sp.dma_start(hT[k:k + 1, 0, 0:D], bias.rearrange("(a d) -> a d", a=1)).then_inc(s_bias, 16)
            sp.dma_start(W[:, :].rearrange("p (r d) -> p r d", d=D),
                         weight.rearrange("r (k p) d -> p (r k) d", p=P)).then_inc(s_w, 16)
            sp.wait_ge(s_tot, 1)
            tail_dma(sp, x, xt, True, s_tail)

            def load_x(lap, k):
                if not (isinstance(lap, int) and lap == 0):
                    sp.wait_ge(s_x[k], 16 * lap)
                sp.dma_start(xr[:, bass.ds(x_slot(lap, k), GW), :],
                             x_groups[bass.ds(lap * XK + k, 1)].rearrange("g p w n -> p (g w) n")
                             ).then_inc(s_x[k], 16)

            for k in range(XK):
                load_x(0, k)
            with sp.Fori(1, XRING) as lap:
                for k in range(XK):
                    load_x(lap, k)

            def store_messages(i, g):
                sp.wait_ge(s_mg, (i * RING + g) * LANES + LANES)
                sp.dma_start(msg_by_lane[:, bass.ds((i * RING + g) * LANES, LANES), :],
                             mg[:, g * LANES:(g + 1) * LANES, :]).then_inc(s_mst[g], 16)

            with sp.Fori(0, LAPS) as i:
                for g in range(RING):
                    store_messages(i, g)

            with sp.Fori(XRING, XLAPS) as lap:
                for k in range(XK):
                    sp.wait_ge(s_out[k], 16 * (lap - XRING + 1))
                    sp.sem_inc(s_held)
                    load_x(lap, k)

            sp.wait_ge(s_win, 1)
            n_over = sp.value_load(over_i[0:1, 0:1], min_val=0, max_val=E)
            with sp.If(n_over > 0):
                sp.wait_ge(s_wmm, NW)
                with sp.Fori(0, NW) as w:
                    with sp.Fori(0, LAPS) as q:
                        sp.wait_ge(s_a_mm, 5 + (w * LAPS + q) * TB)
                        sp.dma_start(xg[:, :, :], msg_by_lane[:, bass.ds(q * TB, TB), :]).then_inc(s_a_msg, 16)

        @block.gpsimd
        def _(pool):
            pool.iota(iota16[:, :], [[1, iota_n]], base=0, channel_multiplier=0,
                      allow_small_or_imprecise_dtypes=True).then_inc(s_iota, 1)
            pool.iota(part[:, :], [[1, 1]], base=0, channel_multiplier=1,
                      allow_small_or_imprecise_dtypes=True).then_inc(s_iota, 1)
            pool.iota(iota_node[:, :, :], [[1, BL], [BL, P]], base=0, channel_multiplier=0,
                      allow_small_or_imprecise_dtypes=True).then_inc(s_iota, 1)

            def gather_x(i, first):
                for g in range(RING):
                    n = i * RING + g
                    if not first:
                        pool.wait_ge(s_gather[g], 16 * LANES * i)
                    pool.tensor_copy(stage1[:, g, :], dst_list[:, bass.ds(n * LANES, LANES)]).then_inc(s_stage, 1)
                    pool.wait_ge(s_stage, n + 1)
                    for k in range(LANES):
                        if not first:
                            pool.wait_ge(s_T, n * LANES + k - TB + 1)
                            pool.sem_inc(s_held)
                        pool.indirect_dma_start(
                            xg[:, g * LANES + k, :], None, x,
                            bass.IndirectOffsetOnAxis(ap=stage1[:, g, k:k + 1], axis=0)).then_inc(s_gather[g], 16)

            pool.wait_ge(s_list, 1)
            gather_x(0, True)
            with pool.Fori(1, LAPS) as i:
                gather_x(i, False)

            H = WB // 2

            def gather_message(w, stage, k):
                pool.indirect_dma_start(
                    gm[:, k, :], None, msg, bass.IndirectOffsetOnAxis(ap=stage, axis=0),
                    bounds_check=ROWS - 1, oob_is_err=False).then_inc(s_wg[k], 16)

            def gather_messages(lap, first):
                for h in range(2):
                    if not first:
                        pool.wait_ge(s_wmm, (lap - 1) * WB + (h + 1) * H)
                    pool.tensor_copy(stage3[:, h, :], row_list[:, bass.ds(lap * WB + h * H, H)]
                                     ).then_inc(s_stage, 1)
                    pool.wait_ge(s_stage, NG + 2 * lap + h + 1)
                    pool.sem_inc(s_held)
                    for j in range(H):
                        k = h * H + j
                        gather_message(lap * WB + k, stage3[:, h, j:j + 1], k)

            pool.wait_ge(s_win, 1)
            for g in range(RING):
                pool.wait_ge(s_mst[g], 16 * LAPS)
            pool.wait_ge(s_zero, 1)
            gather_messages(0, True)
            with pool.Fori(1, XLAPS) as lap:
                gather_messages(lap, False)
            pool.wait_ge(s_wmm, (XLAPS - 1) * WB + 1)
            gather_message(NW - 1, row_list[:, NW - 1:NW], 0)

        @block.scalar
        def _(act):
            act.wait_ge(s_const, 1)

            def normalise(i, j):
                g, k = j // LANES, j % LANES
                n = i * RING + g
                if k == 0:
                    act.wait_ge(s_var, (n + 1) * LANES)
                    nc.scalar.activation(std[:, g, :], mv[:, g, :, 1], ACT.Sqrt, bias=eps[:, 0:1]).then_inc(s_std, 1)
                    act.wait_ge(s_ln, n + 1)
                nc.scalar.activation(xg[:, j, :], xg[:, j, :], ACT.Relu, bias=nmr[:, g, k:k + 1],
                                     scale=rstd[:, g, k:k + 1]).then_inc(s_norm, 1)

            def copy_hT(i, j, first):
                t = i * TB + j
                act.wait_ge(s_T, t + 1)
                if not (first and j < RING):
                    act.wait_ge(s_mm, t - RING + 1)
                nc.scalar.copy(hT[:, j % RING, :], ps_T[j % RING]).then_inc(s_hT, 1)

            def copy_messages(i, j, first):
                t = i * TB + j
                act.wait_ge(s_mm, t + 1)
                if not first and j % LANES == 0:
                    act.wait_ge(s_mst[j // LANES], 16 * i)
                nc.scalar.copy(mg[:, j, :], ps_M[j % RING]).then_inc(s_mg, 1)

            def steps(i, first):
                for j in range(TB):
                    normalise(i, j)
                    for lag, copy in ((2, copy_hT), (4, copy_messages)):
                        if j >= lag:
                            copy(i, j - lag, first)
                        elif not first:
                            copy(i - 1, j - lag + TB, isinstance(i, int) and i == 1)

            steps(0, True)
            steps(1, False)
            with act.Fori(2, LAPS) as i:
                steps(i, False)
            for j in range(TB, TB + 4):
                if j - 2 < TB:
                    copy_hT(LAPS - 1, j - 2, False)
                copy_messages(LAPS - 1, j - 4, False)

            def store_out(lap, k, first):
                act.wait_ge(s_fin, lap * WB + (k + 1) * GW)
                if not first:
                    act.wait_ge(s_out[k], 16 * lap)
                act.dma_start(out_groups[bass.ds(lap * XK + k, 1)].rearrange("g p w n -> p (g w) n"),
                              xr[:, bass.ds(x_slot(lap, k), GW), :]).then_inc(s_out[k], 16)

            for k in range(XK):
                store_out(0, k, True)
            with act.Fori(1, XLAPS) as lap:
                for k in range(XK):
                    store_out(lap, k, False)
            act.wait_ge(s_fin, NW)
            tail_dma(act, out, xt, False, s_outt)
            for k in range(XK):
                act.wait_ge(s_out[k], 16 * XLAPS)
            act.wait_ge(s_outt, 32)

            act.wait_ge(s_win, 1)
            n_over = act.value_load(over_i[0:1, 0:1], min_val=0, max_val=E)
            with act.If(n_over > 0):
                act.dma_start(xr[:, 0, :], x_wins[0]).then_inc(s_a_x, 16)
                with act.Fori(0, NW - 2) as w:
                    act.wait_ge(s_a_win, w + 2)
                    act.dma_start(out_wins[bass.ds(w, 1)].rearrange("w p n -> (w p) n"), xr[:, 0, :]
                                  ).then_inc(s_a_out, 16)
                    act.wait_ge(s_a_out, 16 * (w + 1))
                    act.dma_start(xr[:, 0, :], x_wins[bass.ds(w + 1, 1)].rearrange("w p n -> (w p) n")
                                  ).then_inc(s_a_x, 16)
                act.wait_ge(s_a_win, NW)
                act.dma_start(out_wins[NW - 2], xr[:, 0, :]).then_inc(s_a_out, 16)
                act.wait_ge(s_a_out, 16 * (NW - 1))
                tail_dma(act, x, xr[0:TAILP, 0, :], True, s_a_x)
                act.wait_ge(s_a_win, NW + 1)
                tail_dma(act, out, xr[0:TAILP, 0, :], False, s_a_out)
                act.wait_ge(s_a_out, 16 * (NW + 1))

        @block.tensor
        def _(pe):
            def mm(o, a, b, start=False, stop=False):
                return pe.matmul(o, a, b, start=start, stop=stop, skip_group_check=True)

            pe.wait_ge(s_tot, 1)
            tot = scan[0][:, :, PADC + EC - 1]
            mm(ps_rel, before16[0:EP, 0:EP], tot, True, True)
            mm(ps_cnt, ones16[0:EP, :], tot, True, True).then_inc(s_relps, 1)

            def scatter_dst(n, g, start):
                pe.wait_ge(s_sc, n + 1)
                for c in range(LANES):
                    last = mm(ps_dst, OHL[g][:, c, :], HV[g][:, c, :], start and c == 0)
                last.then_inc(s_scps, 1)

            for g in range(RING):
                scatter_dst(g, g, g == 0)
            with pe.Fori(1, LAPS) as i:
                for g in range(RING):
                    scatter_dst(i * RING + g, g, False)

            pe.wait_ge(s_ohw, 1)
            for n in range(NG):
                for o, a, z in ((ps_L0, 0, 3), (ps_L1, 3, LANES)):
                    last = mm(o, ident16[0:EP, 0:EP],
                              OHW[:, n * LANES + a:n * LANES + z, :].rearrange("p c w -> p (c w)"),
                              n == 0, n == NG - 1)
            last.then_inc(s_lt, 1)
            pe.wait_ge(s_ohw, 2)
            for o, a, z in ((ps_L0, 0, 3), (ps_L1, 3, LANES)):
                mm(o, before16[0:EP, 0:EP], LT[:, a:z, :].rearrange("p l w -> p (l w)"), True)
                for l in range(z - 1):
                    to = max(a, l + 1)
                    last = mm(o[:, (to - a) * NW:(z - a) * NW], ones16[0:EP, 0:EP],
                              LT[:, l:l + 1, :].to_broadcast([EP, z - to, NW]))
            last.then_inc(s_lt, 1)

            def transpose_tile(i, j, first):
                t = i * TB + j
                pe.wait_ge(s_norm, t + 1)
                if not (first and j < RING):
                    pe.wait_ge(s_hT, t - RING + 1)
                for k in range(KC):
                    last = pe.transpose(ps_T[j % RING][:, k * P:(k + 1) * P], xg[:, j, k * P:(k + 1) * P], ident[:, :])
                last.then_inc(s_T, 1)

            def multiply(i, j, first, rel):
                t = i * TB + j
                pe.wait_ge(s_hT, t + 1)
                if not (first and j < RING):
                    pe.wait_ge(s_mg, t - RING + 1)
                for k in range(KC):
                    last = mm(ps_M[j % RING], hT[:, j % RING, k * P:(k + 1) * P],
                              W[:, bass.ds(rel * (KC * D) + k * D, D)], k == 0, k == KC - 1)
                last.then_inc(s_mm, 1)

            def scatter_windows(n, g, start):
                pe.wait_ge(s_rv, n + 1)
                for c in range(LANES):
                    for v in range(2):
                        last = mm(ps_win[:, v * NW:(v + 1) * NW], RV[:, g, c, v, :],
                                  OHW[:, bass.ds(n * LANES + c, 1), :].rearrange("p c w -> p (c w)"),
                                  False)
                last.then_inc(s_rvps, 1)

            def load_rel(i, g):
                packed = pe.value_load(rel_i[0:1, bass.ds(i * RING + g, 1)], min_val=0, max_val=RB ** LANES - 1)
                return [(packed // RB ** k) % RB for k in range(LANES)]

            def body(i, first):
                for g in range(RING):
                    rel = load_rel(i, g)
                    for k in range(LANES + 2):
                        if k < LANES:
                            transpose_tile(i, g * LANES + k, first)
                        if k >= 2:
                            multiply(i, g * LANES + k - 2, first, rel[k - 2])
                    scatter_windows(i * RING + g, g, first and g == 0)

            pe.wait_ge(s_w, 16)
            pe.wait_ge(s_list, 1)
            mm(ps_win, zeros16[0:EP, :], OHW[:, 0:2, :].rearrange("p c w -> p (c w)"), True)
            body(0, True)
            with pe.Fori(1, LAPS) as i:
                body(i, False)
            pe.wait_ge(s_over, 1)
            mm(ps_over, ones16[0:EP, :], over16[:, :], True, True).then_inc(s_overps, 1)

            def sum_window(w, k, s, sel, rows, lap1):
                pw = ps_W[s]
                mm(pw[:, 0:2 * D], ones_b[:, :], bias3[:, :, :].rearrange("p a d -> p (a d)"), True)
                mm(pw[:, 2 * D:3 * D], ones_b[:, :], bias3[:, 0, :], True)
                pe.wait_ge(s_sel, w + 1)
                pe.wait_ge(s_wg[k], 16 * lap1)
                for b in range(BL):
                    last = mm(pw[:, b * D:(b + 1) * D], sel[:, b, :], rows)
                last.then_inc(s_wmm, 1)

            def windows(lap, first):
                for k in range(WB):
                    w = lap * WB + k
                    if not (first and k < 2):
                        pe.wait_ge(s_fin, w - 1)
                    sum_window(w, k, k % 2, S[:, k % 5], gm[:, k, :], lap + 1)

            pe.wait_ge(s_mg, MT)
            windows(0, True)
            with pe.Fori(1, XLAPS) as lap:
                windows(lap, False)
            pe.wait_ge(s_fin, NW - 2)
            sum_window(NW - 1, 0, 0, S[:, 0], gm[:, 0, :], XLAPS + 1)

            pe.wait_ge(s_win, 1)
            n_over = pe.value_load(over_i[0:1, 0:1], min_val=0, max_val=E)
            with pe.If(n_over > 0):
                def scatter_src(c, start):
                    pe.wait_ge(s_a_sc, c + 1)
                    mm(ps_dst, a_lane, a_tile[:, :], start).then_inc(s_a_ps, 1)

                scatter_src(0, True)
                with pe.Fori(1, EC) as c:
                    scatter_src(c, False)
                with pe.Fori(0, NW) as w:
                    pe.wait_ge(s_a_win, w + 1)
                    mm(ps_W[0][:, 0:2 * D], ones_b[:, :], bias3[:, :, :].rearrange("p a d -> p (a d)"), True)
                    mm(ps_W[0][:, 2 * D:3 * D], ones_b[:, :], bias3[:, 0, :], True)
                    with pe.Fori(0, LAPS) as q:
                        pe.wait_ge(s_a_msg, 16 * (w * LAPS + q + 1))
                        for j in range(TB):
                            pe.wait_ge(s_a_sel, (w * LAPS + q) * TB + j + 1)
                            for b in range(BL):
                                last = mm(ps_W[0][:, b * D:(b + 1) * D], S[:, j % 5, b, :], xg[:, j, :])
                            last.then_inc(s_a_mm, 1)

        @block.vector
        def _(dve):
            v = nc.vector
            c = Count(dve, s_dve)

            def ts(o, a, s1, op0, s2=None, op1=None):
                if op1 is None:
                    return v.tensor_scalar(o, a, s1, None, op0)
                return v.tensor_scalar(o, a, s1, s2, op0, op1)

            def stt(o, a, s1, op0, b, op1):
                return v.scalar_tensor_tensor(out=o, in0=a, scalar=s1, in1=b, op0=op0, op1=op1)

            def tt(o, a, b, op):
                return v.tensor_tensor(o, a, b, op)

            def over_cols(a, n):
                return a[:, :, None].to_broadcast([EP, a.shape[1], n])

            def iota_for(n, k):
                return iota16[0:EP, None, 0:n].to_broadcast([EP, k, n])

            v.memset(eps[:], EPS).then_inc(s_const, 1)
            for t, value in ((ones16, 1.0), (zeros16, 0.0), (ones_b, 1.0), (xt, 0.0), (tiles, 0.0)):
                c.up(v.memset(t[:], value))
            for t in (lane16, tile16, win16):
                c.up(v.memset(t, -1.0))
            for t in (dhi16, dlo16, v1, v2):
                c.up(v.memset(t, 0.0))
            for t in scan:
                c.up(v.memset(t[:, :, 0:PADC], 0.0))
            dve.wait_ge(s_iota, 3)
            c.up(ts(ident[:, :], iota16[:, 0:P], part[:, 0:1], ALU.is_equal))
            c.up(ts(ident16[:, :], iota16[:, 0:P], part[:, 0:1], ALU.is_equal))
            done = c.up(ts(before16[:, :], iota16[:, 0:P], part[:, 0:1], ALU.is_gt))

            dve.wait_ge(s_edge, 48)
            c.wait(done)
            c.chain(v.tensor_copy(typ16[:, :], typ_i[:, :]))
            c.chain(tt(scan[2][:, :, PADC:], typ16[:, None, :].to_broadcast([EP, R, EC]),
                       iota16[0:EP, 0:R, None].to_broadcast([EP, R, EC]), ALU.is_equal))
            frm, to, step = scan[2], scan[0], 1
            while step < EC:
                assert step <= PADC
                ins = tt(to[:, :, PADC:], frm[:, :, PADC:], frm[:, :, PADC - step:PADC - step + EC], ALU.add)
                step *= 2
                if step >= EC:
                    ins.then_inc(s_tot, 1)
                    assert to is scan[0]
                else:
                    c.chain(ins)
                    frm, to = to, scan[1] if to is scan[0] else scan[0]

            dve.wait_ge(s_relps, 1)
            c.chain(ts(cnt_i[:, 0, :], ps_cnt, float(P - 1), ALU.add))
            c.chain(ts(cnt_i[:, 1, :], cnt_i[:, 0, :], P.bit_length() - 1, ALU.arith_shift_right))
            c.chain(v.tensor_copy(tiles[:, 0, R:], cnt_i[:, 1, :]))
            frm, to, step = 0, 1, 1
            while step < R:
                c.chain(tt(tiles[:, to, R:], tiles[:, frm, R:], tiles[:, frm, R - step:2 * R - step], ALU.add))
                frm, to, step = to, frm, 2 * step
            first_tile = tiles[:, frm, R - 1:2 * R - 1]
            c.chain(stt(base[:, :], first_tile[0:EP, :], float(P), ALU.mult, ps_rel, ALU.add))
            dve.wait_ge(s_tot, 1)
            c.chain(tt(sc_sum[:, :, :], scan[0][:, :, PADC:], over_cols(base[:, :], EC), ALU.add))
            c.chain(tt(sc_sel[:, :, :], sc_sum[:, :, :], scan[2][:, :, PADC:], ALU.mult))
            c.chain(v.tensor_reduce(pos[:, :], sc_sel[:, :, :].rearrange("p r c -> p c r"), AX_X, ALU.add))
            c.chain(ts(pos_i[:, :], pos[:, :], -1.0, ALU.add))
            c.up(ts(tmp_i[:, 0, :], pos_i[:, :], P - 1, ALU.bitwise_and))
            c.up(ts(tmp_i[:, 1, :], pos_i[:, :], P.bit_length() - 1, ALU.arith_shift_right))
            c.up(ts(tmp_i[:, 2, :], dst_i[:, :], 8, ALU.arith_shift_right))
            c.chain(ts(tmp_i[:, 3, :], dst_i[:, :], 255, ALU.bitwise_and))
            for k, t in enumerate((lane16, tile16, dhi16, dlo16)):
                done = c.up(v.tensor_copy(t[:, 0:EC], tmp_i[:, k, :]))
            c.wait(done)

            def scatter_dst(i, g, first):
                n = i * RING + g
                at = bass.ds(n * LANES, LANES)
                if not first:
                    dve.wait_ge(s_scps, n - RING + 1)
                c.up(tt(OHL[g], iota_for(P, LANES), over_cols(lane16[:, at], P), ALU.is_equal))
                c.chain(tt(OHT[g][:, :, 0:MT], iota_for(MT, LANES), over_cols(tile16[:, at], MT), ALU.is_equal))
                done = c.up(tt(HV[g][:, :, 0:MT], OHT[g][:, :, 0:MT], over_cols(dhi16[:, at], MT), ALU.mult))
                tt(HV[g][:, :, MT:], OHT[g][:, :, 0:MT], over_cols(dlo16[:, at], MT), ALU.mult).then_inc(s_sc, 1)

            for g in range(RING):
                scatter_dst(0, g, True)
            with dve.Fori(1, LAPS) as i:
                c.loop(i - 1, 3 * RING)
                for g in range(RING):
                    scatter_dst(i, g, False)
            c.end(LAPS - 1)

            c.chain(tt(rel_ge[:, :, :], iota16[0:1, 0:MT, None].to_broadcast([1, MT, R]),
                       first_tile[0:1, None, :].to_broadcast([1, MT, R]), ALU.is_ge))
            c.chain(v.tensor_reduce(rel_f[:, :], rel_ge[:, :, :], AX_X, ALU.add))
            c.chain(ts(rel_f[:, :], rel_f[:, :], -1.0, ALU.add))
            digits = rel_f[:, :].rearrange("p (n k) -> p k n", k=LANES)
            acc = digits[:, LANES - 1, :]
            for k in reversed(range(1, LANES - 1)):
                c.chain(stt(rel_p[:, k, :], acc, float(RB), ALU.mult, digits[:, k, :], ALU.add))
                acc = rel_p[:, k, :]
            done = c.up(stt(rel_i[:, :], acc, float(RB), ALU.mult, digits[:, 0, :], ALU.add))
            dve.wait_ge(s_scps, NG)
            c.chain(v.tensor_copy(dlo_f[:, :], ps_dst[:, MT:2 * MT]))
            c.wait(done)
            stt(dst_list[:, :], ps_dst[:, 0:MT], 256.0, ALU.mult, dlo_f[:, :], ALU.add).then_inc(s_list, 1)

            c.chain(ts(tmp_i[:, 4, :], src_i[:, :], 7, ALU.arith_shift_right))
            c.chain(ts(tmp_i[:, 5, :], tmp_i[:, 4, :], float(DIV), ALU.mult))
            c.chain(ts(tmp_i[:, 6, :], tmp_i[:, 5, :], 9, ALU.arith_shift_right))
            c.chain(v.tensor_copy(win16[:, 0:EC], tmp_i[:, 6, :]))
            for n in range(RING):
                a, z = n * ECP // RING, (n + 1) * ECP // RING
                ins = tt(OHW[:, a:z, :], iota_for(NW, z - a), over_cols(win16[:, a:z], NW), ALU.is_equal)
                if n < RING - 1:
                    c.up(ins)
                else:
                    ins.then_inc(s_ohw, 1)
            c.chain(stt(srel[:, :], tmp_i[:, 6, :], float(-WIN), ALU.mult, src_i[:, :], ALU.add))
            c.up(ts(tmp_i[:, 7, :], pos_i[:, :], 7, ALU.bitwise_and))
            c.chain(ts(tmp_i[:, 4, :], pos_i[:, :], 3, ALU.arith_shift_right))
            c.up(ts(v1[:, 0:EC], tmp_i[:, 4, :], 16.0, ALU.add))
            c.chain(stt(v2f[:, :], tmp_i[:, 7, :], 512.0, ALU.mult, srel[:, :], ALU.add))
            c.chain(ts(v2[:, 0:EC], v2f[:, :], -2048.0, ALU.add))
            dve.wait_ge(s_lt, 1)
            c.chain(v.tensor_copy(LT[:, 0:3, :].rearrange("p l w -> p (l w)"), ps_L0))
            v.tensor_copy(LT[:, 3:, :].rearrange("p l w -> p (l w)"), ps_L1).then_inc(s_ohw, 1)
            dve.wait_ge(s_bias, 48)
            c.chain(v.tensor_copy(bias_part[:, 0, :], bias_row))
            c.chain(tt(bias_rest[:, 0, :], bias_row, bias_part[:, 0, :], ALU.subtract))
            c.chain(v.tensor_copy(bias_part[:, 1, :], bias_rest[:, 0, :]))
            c.chain(tt(bias_rest[:, 1, :], bias_rest[:, 0, :], bias_part[:, 1, :], ALU.subtract))
            c.chain(v.tensor_copy(bias_part[:, 2, :], bias_rest[:, 1, :]))
            c.chain(ts(bias_sel[:, 0, :], bias_part[:, 0, :], ident[0:3, 0:1], ALU.mult))
            c.chain(stt(bias_sel[:, 1, :], bias_part[:, 1, :], ident[0:3, 1:2], ALU.mult, bias_sel[:, 0, :], ALU.add))
            for k in range(2):
                c.up(stt(bias3[:, k, :], bias_part[:, 2, :], ident[0:3, 2:3], ALU.mult, bias_sel[:, 1, :], ALU.add))
            v.memset(scratch[:, 0:WB * D], 0.0).then_inc(s_zero, 1)
            dve.wait_ge(s_lt, 2)
            c.up(v.tensor_copy(C[:, 0:3, :].rearrange("p l w -> p (l w)"), ps_L0))
            c.chain(v.tensor_copy(C[:, 3:, :].rearrange("p l w -> p (l w)"), ps_L1))

            def group(i, g, first):
                n = i * RING + g
                at = bass.ds(n * LANES, LANES)
                ohw = OHW[:, at, :]
                dve.wait_ge(s_gather[g], 16 * LANES * (i + 1))
                for k in range(LANES):
                    c.up(v.bn_stats(stats[:, g, k, :], xg[:, g * LANES + k, :]))
                c.chain(tt(prod[:, :, :], ohw, C[:, :, :], ALU.mult))
                with nc.allow_low_precision(reason="one term is not zero; whole numbers, exact up to 2048"):
                    c.up(v.tensor_reduce(rank16[:, at], prod[:, :, :], AX_X, ALU.add))
                for k in range(LANES):
                    v.bn_aggr(mv[:, g, k, :], stats[:, g, k, :]).then_inc(s_var, 1)
                c.up(tt(C[:, :, :], C[:, :, :], ohw, ALU.add))
                dve.wait_ge(s_std, n + 1)
                c.chain(v.reciprocal(rstd[:, g, :], std[:, g, :]))
                if not first:
                    dve.wait_ge(s_rvps, n - RING + 1)
                c.up(tt(OHR[:, g, :, :], iota_for(P, LANES), over_cols(rank16[:, at], P), ALU.is_equal))
                stt(nmr[:, g, :], mv[:, g, :, 0], -1.0, ALU.mult, rstd[:, g, :], ALU.mult).then_inc(s_ln, 1)
                c.wait(c.base + c.n)
                c.chain(tt(RV[:, g, :, 0, :], OHR[:, g, :, :], over_cols(v1[:, at], P), ALU.mult))
                tt(RV[:, g, :, 1, :], OHR[:, g, :, :], over_cols(v2[:, at], P), ALU.mult).then_inc(s_rv, 1)

            PER = RING * (LANES + 6)
            for g in range(RING):
                group(0, g, True)
            with dve.Fori(1, LAPS) as i:
                c.loop(i - 1, PER)
                for g in range(RING):
                    group(i, g, False)
            c.end(LAPS - 1)

            c.chain(ts(over[:, :], rank16[:, :], float(P), ALU.is_ge))
            c.chain(v.tensor_reduce(over_n[:, :], over[:, :], AX_X, ALU.add))
            v.tensor_copy(over16[:, :], over_n[:, :]).then_inc(s_over, 1)
            dve.wait_ge(s_overps, 1)
            c.up(v.tensor_copy(over_i[:, :], ps_over))
            dve.wait_ge(s_rvps, NG)
            c.chain(v.tensor_copy(li[:, 0, :], ps_win[:, 0:NW]))
            c.up(ts(li[:, 1, :], ps_win[:, NW:2 * NW], 2048.0, ALU.add))
            c.chain(ts(empty, ps_win[:, 0:NW], 0.5, ALU.is_lt))
            c.up(ts(li[:, 2, :], li[:, 0, :], 4, ALU.arith_shift_right))
            c.up(ts(li[:, 3, :], li[:, 0, :], 15, ALU.bitwise_and))
            c.up(ts(li[:, 4, :], li[:, 1, :], 9, ALU.arith_shift_right))
            c.chain(ts(li[:, 5, :], li[:, 1, :], 511, ALU.bitwise_and))
            c.up(stt(src_list[:, :], empty, -1024.0, ALU.mult, li[:, 5, :], ALU.add))
            c.chain(stt(row_f[:, 0, :], li[:, 3, :], 8.0, ALU.mult, li[:, 4, :], ALU.add))
            c.chain(stt(row_f[:, 1, :], row_f[:, 0, :], float(MT), ALU.mult, li[:, 2, :], ALU.add))
            c.chain(ts(lv, row_f[:, 1, :], -1.0, ALU.add))
            stt(row_list[:, :], empty, float(NONE), ALU.mult, lv, ALU.add).then_inc(s_win, 1)
            dve.wait_ge(s_win, 1)

            def select(lap, k, first):
                w = lap * WB + k
                if not (first and k < 5):
                    dve.wait_ge(s_wmm, w - 4)
                ts(S[:, k % 5], iota_node[:, :, :], src_list[:, bass.ds(w, 1)], ALU.is_equal).then_inc(s_sel, 1)

            def finish(lap, k):
                w = lap * WB + k
                dve.wait_ge(s_wmm, w + 1)
                if k % GW == 0:
                    dve.wait_ge(s_x[k // GW], 16 * (lap + 1))
                xs = xr[:, bass.ds(x_slot(lap, 0) + k, 1), :].rearrange("p w n -> p (w n)")
                stt(xs, ps_W[k % 2], 0.0, ALU.max, xs, ALU.add).then_inc(s_fin, 1)

            def windows(lap, first):
                for k in range(2):
                    select(lap, k, first)
                for k in range(WB):
                    finish(lap, k)
                    if k + 2 < WB:
                        select(lap, k + 2, first)

            windows(0, True)
            with dve.Fori(1, XLAPS) as lap:
                windows(lap, False)
            select(XLAPS, 0, False)
            dve.wait_ge(s_wmm, NW)
            dve.wait_ge(s_tail, 32)
            stt(xt[:, :], ps_W[0][0:TAILP, :], 0.0, ALU.max, xt[:, :], ALU.add).then_inc(s_fin, 1)

            n_over = dve.value_load(over_i[0:1, 0:1], min_val=0, max_val=E)
            with dve.If(n_over > 0):
                dve.wait_ge(s_fin, NW)
                c.up(ts(tmp_i[:, 0, :], src_i[:, :], 8, ALU.arith_shift_right))
                c.chain(ts(tmp_i[:, 1, :], src_i[:, :], 255, ALU.bitwise_and))
                c.up(ts(a_val[:, 0, :], tmp_i[:, 0, :], 1.0, ALU.add))
                c.chain(v.tensor_copy(a_val[:, 1, :], tmp_i[:, 1, :]))
                c.chain(v.tensor_copy(a_pos[:, 0, :], lane16[:, 0:EC]))
                c.chain(v.tensor_copy(a_pos[:, 1, :], tile16[:, 0:EC]))

                def scatter_src(col, first):
                    one = bass.ds(col, 1)
                    if not first:
                        dve.wait_ge(s_a_ps, col)
                    c.up(ts(a_lane, iota16[0:EP, 0:P], a_pos[:, 0, one], ALU.is_equal))
                    c.chain(ts(a_tile[:, 0:MT], iota16[0:EP, 0:MT], a_pos[:, 1, one], ALU.is_equal,
                               a_val[:, 0, one], ALU.mult))
                    ts(a_tile[:, MT:2 * MT], iota16[0:EP, 0:MT], a_pos[:, 1, one], ALU.is_equal,
                       a_val[:, 1, one], ALU.mult).then_inc(s_a_sc, 1)

                scatter_src(0, True)
                with dve.Fori(1, EC) as col:
                    c.loop(col - 1, 2)
                    scatter_src(col, False)
                c.end(EC - 1)
                dve.wait_ge(s_a_ps, EC)
                c.chain(ts(dlo_f[:, :], ps_dst[:, MT:2 * MT], -256.0, ALU.add))
                c.chain(stt(src_slot[:, :], ps_dst[:, 0:MT], 256.0, ALU.mult, dlo_f[:, :], ALU.add))
                v.memset(over[:, 0:1], 0.0).then_inc(s_a_mm, 5)
                v.memset(over16[:, :], 0.0).then_inc(s_a_win, 1)

                def window(w, parts, done_x):
                    with dve.Fori(0, LAPS) as q:
                        for j in range(TB):
                            dve.wait_ge(s_a_mm, (w * LAPS + q) * TB + j + 1)
                            ts(S[:, j % 5], iota_node[:, :, :], src_slot[:, bass.ds(q * TB + j, 1)],
                               ALU.is_equal).then_inc(s_a_sel, 1)
                    dve.wait_ge(s_a_mm, 5 + (w + 1) * MT)
                    c.chain(ts(src_slot[:, :], src_slot[:, :], float(-WIN), ALU.add))
                    dve.wait_ge(s_a_x, done_x)
                    stt(xr[0:parts, 0, :], ps_W[0][0:parts, :], 0.0, ALU.max, xr[0:parts, 0, :],
                        ALU.add).then_inc(s_a_win, 1)

                with dve.Fori(0, NW - 1) as w:
                    c.loop(w, 1)
                    window(w, P, 16 * (w + 1))
                c.end(NW - 1)
                window(NW - 1, TAILP, 16 * (NW + 1))


_INS = ["x", "src", "dst", "edge_type_8", "L0_gnn_weight", "L0_gnn_bias"]


def kernel(**inputs):
    import numpy as _np
    import concourse.bacc as _bacc
    from concourse import mybir as _mybir
    from concourse.bass_utils import run_bass_kernel_spmd as _run

    nc = _bacc.Bacc("TRN2", target_bir_lowering=False, num_devices=1)
    arrays, args = {}, []
    for name in _INS:
        a = _np.ascontiguousarray(inputs[name])
        arrays[f"in_{name}"] = a
        args.append(nc.dram_tensor(f"in_{name}", a.shape, _mybir.dt.from_np(a.dtype), kind="ExternalInput").ap())
    shape = arrays["in_x"].shape
    args.append(nc.dram_tensor("out_0", shape, _mybir.dt.float32, kind="ExternalOutput").ap())
    gnn_kernel(nc, *args)
    r = _run(nc, [arrays], core_ids=[0])
    return r.results[0]["out_0"]
```

```python
from contextlib import ExitStack

import concourse.bass as bass
from concourse import mybir
from concourse.alu_op_type import AluOpType as ALU

P = 128
ACT = mybir.ActivationFunctionType
AX_X = mybir.AxisListType.X
F32 = mybir.dt.float32
F16 = mybir.dt.float16
BF16 = mybir.dt.bfloat16
I32 = mybir.dt.int32
EPS = 1e-5


class Count:

    def __init__(self, eng, sem):
        self.eng, self.sem, self.base, self.n, self.per, self.saved = eng, sem, 0, 0, 0, 0

    def up(self, ins):
        ins.then_inc(self.sem, 1)
        self.n += 1
        return self.base + self.n

    def wait(self, value):
        self.eng.wait_ge(self.sem, value)

    def chain(self, ins):
        self.wait(self.up(ins))

    def loop(self, i, per):
        self.saved, self.per = self.n, per
        self.base, self.n = i * per + self.n, 0

    def end(self, trips):
        assert self.n == self.per, (self.n, self.per)
        self.base, self.n = 0, self.saved + trips * self.per


def gnn_kernel(nc, x, src, dst, edge_type, weight, bias, out):
    NODES, D = x.shape
    E = src.shape[0]
    R = weight.shape[0]
    KC = D // P
    EP = max(p for p in range(1, P + 1) if E % p == 0)
    EC = E // EP
    MT = (E - R) // P + R
    LANES = 5
    RING = 3
    NG = MT // LANES
    LAPS = NG // RING
    ECP = NG * LANES
    TB = LANES * RING
    assert MT == NG * LANES and NG == LAPS * RING and EC <= ECP and EP <= P
    BL = 3
    WIN = BL * P
    NW = -(-NODES // WIN)
    GW = 2
    XK = 5
    WB = GW * XK
    XLAPS = (NW - 1) // WB
    XRING = 3
    TAIL = NODES - (NW - 1) * WIN
    TAILP = -(-TAIL // BL)
    TAILF = TAIL // BL
    assert NW - 1 == XLAPS * WB and 0 < TAIL < WIN and XLAPS > XRING
    assert TAILP > TAILF
    ROWS = MT * P
    NONE = 1 << 17
    assert ROWS // 8 + 16 <= 2048 and WIN <= 512 and NODES < 1 << 16
    RB = 8
    assert R <= RB
    DIV = 171
    assert BL == 3 and NODES >> 7 < 512
    W0 = 512 // LANES
    GC = LANES + LANES % 2

    msg = nc.dram_tensor("messages", (ROWS, D), F32, kind="Internal").ap()
    msg_by_lane = msg.rearrange("(p t) d -> p t d", t=MT)

    with ExitStack() as ctx:
        def sb(name, shape, dt):
            return ctx.enter_context(nc.sbuf_tensor(name, shape, dt))

        def sem(name):
            return ctx.enter_context(nc.semaphore(name))

        iota_n = max(P, MT, NW)
        iota16 = sb("iota16", [P, iota_n], F16)
        iota_c = sb("iota_c", [P, iota_n, LANES], F16)
        iota_node = sb("iota_node", [P, BL, P], F32)
        part = sb("part", [P, 1], F32)
        ident = sb("ident", [P, P], F32)
        ident16 = sb("ident16", [P, P], F16)
        before16 = sb("before16", [P, P], F16)
        ones16 = sb("ones16", [P, P], F16)
        eps = sb("eps", [P, 1], F32)
        zeros16 = sb("zeros16", [P, P], F16)
        ones_b = sb("ones_b", [3, P], BF16)
        bias3 = sb("bias3", [3, 2, D], BF16)
        W = sb("W", [P, R * KC * D], F32)

        typ_i = sb("typ_i", [EP, EC], I32)
        dst_i = sb("dst_i", [EP, EC], I32)
        src_i = sb("src_i", [EP, EC], I32)
        typ16 = sb("typ16", [EP, EC], F16)
        tmp_i = sb("tmp_i", [EP, 8, EC], I32)
        pos = sb("pos", [EP, EC], F32)
        pos_i = sb("pos_i", [EP, EC], I32)
        srel = sb("srel", [EP, EC], F32)
        v2f = sb("v2f", [EP, EC], F32)
        cols = sb("cols", [EP, 7, NG, GC], F16)
        lane16, tile16, win16, dhi16, dlo16, v1, v2 = (cols[:, k, :, :] for k in range(7))
        rank16 = sb("rank16", [EP, NG, GC], F16)
        over = sb("over", [EP, NG, GC], F16)
        over_n = sb("over_n", [EP, 1], F32)
        over16 = sb("over16", [EP, 1], F16)
        over_i = sb("over_i", [P, 1], I32)
        base = sb("base", [EP, R], F32)
        cnt_i = sb("cnt_i", [P, 2, R], I32)
        tiles = sb("tiles", [P, 2, 2 * R], F32)
        rel_ge = sb("rel_ge", [1, MT, R], F32)
        rel_f = sb("rel_f", [1, MT], F32)
        rel_p = sb("rel_p", [1, LANES, NG], F32)
        rel_i = sb("rel_i", [1, NG], I32)
        dlo_f = sb("dlo_f", [P, MT], F32)
        dst_list = sb("dst_list", [P, MT], I32)
        OHW = sb("OHW", [EP, NG, NW, LANES], F16)
        LT = sb("LT", [EP, NW, LANES], F16)
        C = sb("C", [EP, NW, LANES], F16)
        prod = sb("prod", [EP, NW, LANES], F16)
        RW = RING * 3 * P * LANES // 2
        ranks = sb("ranks", [P, RW], F32)
        RV = [ranks[0:EP, g * P * LANES:(g + 1) * P * LANES].bitcast(F16)
              .rearrange("p (v r c) -> p v r c", v=2, c=LANES) for g in range(RING)]
        OHR = [ranks[0:EP, (2 * RING + g) * P * LANES // 2:(2 * RING + g + 1) * P * LANES // 2].bitcast(F16)
               .rearrange("p (r c) -> p r c", c=LANES) for g in range(RING)]

        row_list = sb("row_list", [P, NW], I32)
        src_list = sb("src_list", [P, NW], F32)

        xg = sb("xg", [P, TB, D], F32)
        mg = sb("mg", [P, TB, D], F32)
        hT = sb("hT", [P, RING, KC * P], F32)
        stage1 = sb("stage1", [P, RING, LANES], I32)
        stats = sb("stats", [P, RING, LANES, 6], F32)
        mv = sb("mv", [P, RING, LANES, 2], F32)
        std = sb("std", [P, RING, LANES], F32)
        rstd = sb("rstd", [P, RING, LANES], F32)
        nmr = sb("nmr", [P, RING, LANES], F32)

        PADC = 64
        mg_flat = mg[:, :, :].rearrange("p t d -> p (t d)")
        xg_flat = xg[:, :, :].rearrange("p t d -> p (t d)")
        sc_sum, sc_sel = (mg_flat[0:EP, k * R * EC:(k + 1) * R * EC].rearrange("p (r c) -> p r c", r=R)
                          for k in range(2))
        scan_w = R * (PADC + EC) // 2
        at = 2 * R * EC
        scan = [mg_flat[0:EP, at + k * scan_w:at + (k + 1) * scan_w].bitcast(F16)
                .rearrange("p (r c) -> p r c", r=R) for k in range(3)]
        assert at + 3 * scan_w <= TB * D
        at = 0
        OHL, OHT, HV = [], [], []
        for g in range(RING):
            for lst, n in ((OHL, P), (OHT, MT + 1), (HV, 2 * MT)):
                w = LANES * n // 2
                lst.append(xg_flat[0:EP, at:at + w].bitcast(F16).rearrange("p (n c) -> p n c", c=LANES))
                at += w
        assert at <= TB * D
        bias_part, bias_sel = (mg_flat[0:3, a * D:a * D + n * D // 2].bitcast(BF16).rearrange("p (k d) -> p k d", d=D)
                               for a, n in ((0, 3), (2, 2)))
        bias_row = hT[0:3, 0, 0:D]
        bias_rest = hT[0:3, 1:3, 0:D]
        gm = xg
        SS = 5
        S = ranks[:, 0:SS * WIN].rearrange("p (s b n) -> p s b n", s=SS, b=BL)
        li_f = ranks[:, SS * WIN:SS * WIN + 7 * NW].rearrange("p (k w) -> p k w", w=NW)
        li = li_f.bitcast(I32)
        assert WB <= TB and SS * WIN + 7 * NW <= RW
        stage3 = sb("stage3", [P, 2, WB // 2], I32)
        XS = XRING * XK
        xr = sb("xr", [P, XS * GW, BL * D], F32)
        xt = sb("xt", [TAILP, BL * D], F32)

        a_val, a_pos = (mg[0:EP, k, 0:2 * EC].rearrange("p (k c) -> p k c", k=2) for k in range(2))
        a_lane = OHR[0].rearrange("p r c -> p (r c)")[:, 0:P]
        a_tile = OHW[:, 0, :, :].rearrange("p w c -> p (w c)")[:, 0:2 * MT]
        src_slot = mg[:, 2, 0:MT]

        ps = ctx.enter_context(nc.psum_tensor("ps", [P, 8 * 512], F32))

        def bank(b, a, z, parts=P):
            return ps[0:parts, 512 * b + a:512 * b + z]

        ps_T = [bank(b, 0, KC * P) for b in (0, 1, 4)]
        ps_M = [bank(b, 0, D) for b in (2, 3, 5)]
        ps_L = [(bank(6, 0, W0 * LANES, EP).rearrange("p (w l) -> p w l", l=LANES), slice(0, W0)),
                (bank(7, 0, (NW - W0) * LANES, EP).rearrange("p (w l) -> p w l", l=LANES), slice(W0, NW))]
        ps_dst = bank(6, 0, 2 * MT)
        ps_over = bank(6, 0, 1)
        ps_rel = bank(7, 0, R, EP)
        ps_cnt = bank(7, R, 2 * R)
        ps_win = bank(7, 0, 2 * NW)
        ps_W = [ps[:, 1024 * k:1024 * k + BL * D] for k in range(2)]
        assert (NW - W0) * LANES <= 512 and 2 * MT <= 512 and BL * D <= 1024

        s_edge = sem("s_edge")
        s_bias = sem("s_bias")
        s_w = sem("s_w")
        s_tail = sem("s_tail")
        s_iota = sem("s_iota")
        s_dve = sem("s_dve")
        s_const = sem("s_const")
        s_tot = sem("s_tot")
        s_relps = sem("s_relps")
        s_sc = sem("s_sc")
        s_scps = sem("s_scps")
        s_dstps = sem("s_dstps")
        s_list = sem("s_list")
        s_ohw = sem("s_ohw")
        s_lt = sem("s_lt")
        s_stage = sem("s_stage")
        s_gather = [sem(f"s_gather{g}") for g in range(RING)]
        s_var = sem("s_var")
        s_std = sem("s_std")
        s_ln = sem("s_ln")
        s_norm = sem("s_norm")
        s_T = sem("s_T")
        s_hT = sem("s_hT")
        s_mm = sem("s_mm")
        s_mg = sem("s_mg")
        s_mst = [sem(f"s_mst{g}") for g in range(RING)]
        s_rv = sem("s_rv")
        s_rvps = sem("s_rvps")
        s_held = sem("s_held")
        s_win = sem("s_win")
        s_overps = sem("s_overps")
        s_over = sem("s_over")
        s_wg = [sem(f"s_wg{k}") for k in range(WB)]
        s_sel = sem("s_sel")
        s_wmm = sem("s_wmm")
        s_fin = sem("s_fin")
        s_x = [sem(f"s_x{k}") for k in range(XK)]
        s_out = [sem(f"s_out{k}") for k in range(XK)]
        s_outt = sem("s_outt")
        s_a_sc = sem("s_a_sc")
        s_a_ps = sem("s_a_ps")
        s_a_list = sem("s_a_list")
        s_a_msg = sem("s_a_msg")
        s_a_sel = sem("s_a_sel")
        s_a_mm = sem("s_a_mm")
        s_a_win = sem("s_a_win")
        s_a_x = sem("s_a_x")
        s_a_out = sem("s_a_out")

        x_groups = x[0:XLAPS * WB * WIN, :].rearrange("(g w p b) d -> g p w (b d)", w=GW, p=P, b=BL)
        out_groups = out[0:XLAPS * WB * WIN, :].rearrange("(g w p b) d -> g p w (b d)", w=GW, p=P, b=BL)
        x_wins = x[0:XLAPS * WB * WIN, :].rearrange("(w p b) d -> w p (b d)", p=P, b=BL)
        out_wins = out[0:XLAPS * WB * WIN, :].rearrange("(w p b) d -> w p (b d)", p=P, b=BL)
        t0 = (NW - 1) * WIN
        tail_full = slice(t0, t0 + TAILF * BL)
        tail_rest = slice(t0 + TAILF * BL, NODES)
        REST = NODES - tail_rest.start

        def tail_dma(eng, dram, tile, load, done):
            full = dram[tail_full, :].rearrange("(p b) d -> p (b d)", b=BL)
            rest = dram[tail_rest, :].rearrange("(p b) d -> p (b d)", b=REST)
            for d, s in ((full, tile[0:TAILF, :]), (rest, tile[TAILF:TAILP, 0:REST * D])):
                eng.dma_start(*((s, d) if load else (d, s))).then_inc(done, 16)

        def x_slot(lap, k):
            return (lap % XRING) * WB + k * GW

        block = ctx.enter_context(nc.Block())

        @block.sync
        def _(sp):
            for t, d in ((typ_i, edge_type), (dst_i, dst), (src_i, src)):
                sp.dma_start(t[:, :], d.rearrange("(p c) -> p c", c=EC)).then_inc(s_edge, 16)
            for k in range(3):
                sp.dma_start(hT[k:k + 1, 0, 0:D], bias.rearrange("(a d) -> a d", a=1)).then_inc(s_bias, 16)
            sp.dma_start(W[:, :].rearrange("p (r d) -> p r d", d=D),
                         weight.rearrange("r (k p) d -> p (r k) d", p=P)).then_inc(s_w, 16)
            sp.wait_ge(s_tot, 1)
            tail_dma(sp, x, xt, True, s_tail)

            def load_x(lap, k):
                if not (isinstance(lap, int) and lap == 0):
                    sp.wait_ge(s_x[k], 16 * lap)
                sp.dma_start(xr[:, bass.ds(x_slot(lap, k), GW), :],
                             x_groups[bass.ds(lap * XK + k, 1)].rearrange("g p w n -> p (g w) n")
                             ).then_inc(s_x[k], 16)

            for k in range(XK):
                load_x(0, k)
            with sp.Fori(1, XRING) as lap:
                for k in range(XK):
                    load_x(lap, k)

            def store_messages(i, g):
                sp.wait_ge(s_mg, (i * RING + g) * LANES + LANES)
                sp.dma_start(msg_by_lane[:, bass.ds((i * RING + g) * LANES, LANES), :],
                             mg[:, g * LANES:(g + 1) * LANES, :]).then_inc(s_mst[g], 16)

            with sp.Fori(0, LAPS) as i:
                for g in range(RING):
                    store_messages(i, g)

            with sp.Fori(XRING, XLAPS) as lap:
                for k in range(XK):
                    sp.wait_ge(s_out[k], 16 * (lap - XRING + 1))
                    sp.sem_inc(s_held)
                    load_x(lap, k)

            sp.wait_ge(s_win, 1)
            n_over = sp.value_load(over_i[0:1, 0:1], min_val=0, max_val=E)
            with sp.If(n_over > 0):
                sp.wait_ge(s_wmm, NW)
                with sp.Fori(0, NW) as w:
                    with sp.Fori(0, LAPS) as q:
                        sp.wait_ge(s_a_mm, SS + (w * LAPS + q) * TB)
                        sp.dma_start(xg[:, :, :], msg_by_lane[:, bass.ds(q * TB, TB), :]).then_inc(s_a_msg, 16)

        @block.gpsimd
        def _(pool):
            pool.iota(iota16[:, :], [[1, iota_n]], base=0, channel_multiplier=0,
                      allow_small_or_imprecise_dtypes=True).then_inc(s_iota, 1)
            pool.iota(part[:, :], [[1, 1]], base=0, channel_multiplier=1,
                      allow_small_or_imprecise_dtypes=True).then_inc(s_iota, 1)
            pool.iota(iota_node[:, :, :], [[1, BL], [BL, P]], base=0, channel_multiplier=0,
                      allow_small_or_imprecise_dtypes=True).then_inc(s_iota, 1)

            def gather_x(i, first):
                for g in range(RING):
                    n = i * RING + g
                    if not first:
                        pool.wait_ge(s_gather[g], 16 * LANES * i)
                    pool.tensor_copy(stage1[:, g, :], dst_list[:, bass.ds(n * LANES, LANES)]).then_inc(s_stage, 1)
                    pool.wait_ge(s_stage, n + 1)
                    for k in range(LANES):
                        if not first:
                            pool.wait_ge(s_T, n * LANES + k - TB + 1)
                            pool.sem_inc(s_held)
                        pool.indirect_dma_start(
                            xg[:, g * LANES + k, :], None, x,
                            bass.IndirectOffsetOnAxis(ap=stage1[:, g, k:k + 1], axis=0)).then_inc(s_gather[g], 16)

            pool.wait_ge(s_list, 1)
            gather_x(0, True)
            with pool.Fori(1, LAPS) as i:
                gather_x(i, False)

            H = WB // 2

            def gather_message(w, stage, k):
                pool.indirect_dma_start(
                    gm[:, k, :], None, msg, bass.IndirectOffsetOnAxis(ap=stage, axis=0),
                    bounds_check=ROWS - 1, oob_is_err=False).then_inc(s_wg[k], 16)

            def gather_messages(lap, first):
                for h in range(2):
                    if not first:
                        pool.wait_ge(s_wmm, (lap - 1) * WB + (h + 1) * H)
                    pool.tensor_copy(stage3[:, h, :], row_list[:, bass.ds(lap * WB + h * H, H)]
                                     ).then_inc(s_stage, 1)
                    pool.wait_ge(s_stage, NG + 2 * lap + h + 1)
                    pool.sem_inc(s_held)
                    for j in range(H):
                        k = h * H + j
                        gather_message(lap * WB + k, stage3[:, h, j:j + 1], k)

            pool.wait_ge(s_win, 1)
            for g in range(RING):
                pool.wait_ge(s_mst[g], 16 * LAPS)
            pool.wait_ge(s_T, MT)
            gather_messages(0, True)
            with pool.Fori(1, XLAPS) as lap:
                gather_messages(lap, False)
            pool.wait_ge(s_wmm, (XLAPS - 1) * WB + 1)
            gather_message(NW - 1, row_list[:, NW - 1:NW], 0)

        @block.scalar
        def _(act):
            act.wait_ge(s_const, 1)

            def deviations(i, g):
                act.wait_ge(s_var, (i * RING + g + 1) * LANES)
                nc.scalar.activation(std[:, g, :], mv[:, g, :, 1], ACT.Sqrt, bias=eps[:, 0:1]).then_inc(s_std, 1)

            def normalise(i, j, first):
                g, k = j // LANES, j % LANES
                if k == 0:
                    act.wait_ge(s_ln, i * RING + g + 1)
                nc.scalar.activation(xg[:, j, :], xg[:, j, :], ACT.Relu, bias=nmr[:, g, k:k + 1],
                                     scale=rstd[:, g, k:k + 1]).then_inc(s_norm, 1)

            def copy_hT(i, j, first):
                t = i * TB + j
                act.wait_ge(s_T, t + 1)
                if not (first and j < RING):
                    act.wait_ge(s_mm, t - RING + 1)
                nc.scalar.copy(hT[:, j % RING, :], ps_T[j % RING]).then_inc(s_hT, 1)

            def copy_messages(i, j, first):
                t = i * TB + j
                act.wait_ge(s_mm, t + 1)
                if not first and j % LANES == 0:
                    act.wait_ge(s_mst[j // LANES], 16 * i)
                nc.scalar.copy(mg[:, j, :], ps_M[j % RING]).then_inc(s_mg, 1)

            LAGS = ((3, normalise), (5, copy_hT), (7, copy_messages))

            def steps(i, first, second=False):
                for j in range(TB):
                    if j % LANES == 0:
                        deviations(i, j // LANES)
                    for lag, do in LAGS:
                        if j >= lag:
                            do(i, j - lag, first)
                        elif not first:
                            do(i - 1, j - lag + TB, second)

            steps(0, True)
            steps(1, False, True)
            with act.Fori(2, LAPS) as i:
                steps(i, False)
            for j in range(TB, TB + LAGS[-1][0]):
                for lag, do in LAGS:
                    if j - lag < TB:
                        do(LAPS - 1, j - lag, False)

            def store_out(lap, k, first):
                act.wait_ge(s_fin, lap * WB + (k + 1) * GW)
                if not first:
                    act.wait_ge(s_out[k], 16 * lap)
                act.dma_start(out_groups[bass.ds(lap * XK + k, 1)].rearrange("g p w n -> p (g w) n"),
                              xr[:, bass.ds(x_slot(lap, k), GW), :]).then_inc(s_out[k], 16)

            for k in range(XK):
                store_out(0, k, True)
            with act.Fori(1, XLAPS) as lap:
                for k in range(XK):
                    store_out(lap, k, False)
            act.wait_ge(s_fin, NW)
            tail_dma(act, out, xt, False, s_outt)
            for k in range(XK):
                act.wait_ge(s_out[k], 16 * XLAPS)
            act.wait_ge(s_outt, 32)

            act.wait_ge(s_win, 1)
            n_over = act.value_load(over_i[0:1, 0:1], min_val=0, max_val=E)
            with act.If(n_over > 0):
                act.dma_start(xr[:, 0, :], x_wins[0]).then_inc(s_a_x, 16)
                with act.Fori(0, NW - 2) as w:
                    act.wait_ge(s_a_win, w + 2)
                    act.dma_start(out_wins[bass.ds(w, 1)].rearrange("w p n -> (w p) n"), xr[:, 0, :]
                                  ).then_inc(s_a_out, 16)
                    act.wait_ge(s_a_out, 16 * (w + 1))
                    act.dma_start(xr[:, 0, :], x_wins[bass.ds(w + 1, 1)].rearrange("w p n -> (w p) n")
                                  ).then_inc(s_a_x, 16)
                act.wait_ge(s_a_win, NW)
                act.dma_start(out_wins[NW - 2], xr[:, 0, :]).then_inc(s_a_out, 16)
                act.wait_ge(s_a_out, 16 * (NW - 1))
                tail_dma(act, x, xr[0:TAILP, 0, :], True, s_a_x)
                act.wait_ge(s_a_win, NW + 1)
                tail_dma(act, out, xr[0:TAILP, 0, :], False, s_a_out)
                act.wait_ge(s_a_out, 16 * (NW + 1))

        @block.tensor
        def _(pe):
            def mm(o, a, b, start=False, stop=False):
                return pe.matmul(o, a, b, start=start, stop=stop, skip_group_check=True)

            pe.wait_ge(s_tot, 1)
            tot = scan[0][:, :, PADC + EC - 1]
            mm(ps_rel, before16[0:EP, 0:EP], tot, True, True)
            mm(ps_cnt, ones16[0:EP, :], tot, True, True).then_inc(s_relps, 1)

            def scatter_dst(n, g, start):
                pe.wait_ge(s_sc, n + 1)
                for c in range(LANES):
                    last = mm(ps_dst, OHL[g][:, :, c], HV[g][:, :, c], start and c == 0)
                last.then_inc(s_scps, 1)

            for g in range(RING):
                scatter_dst(g, g, g == 0)
            with pe.Fori(1, LAPS) as i:
                for g in range(RING):
                    scatter_dst(i * RING + g, g, False)

            third = NG // RING

            def count_lanes(k):
                pe.wait_ge(s_ohw, k + 1)
                for n in range(k * third, (k + 1) * third):
                    for o, ws in ps_L:
                        last = mm(o, ident16[0:EP, 0:EP], OHW[:, n, ws, :], n == 0, n == NG - 1)
                if k == RING - 1:
                    last.then_inc(s_lt, 1)

            def first_ranks():
                pe.wait_ge(s_ohw, RING + 1)
                for o, ws in ps_L:
                    mm(o, before16[0:EP, 0:EP], LT[:, ws, :], True)
                    for l in range(LANES - 1):
                        to = LANES - 1 - l
                        last = mm(o[:, :, l + 1:LANES], ones16[0:EP, 0:EP],
                                  LT[:, ws, l:l + 1].to_broadcast([EP, ws.stop - ws.start, to]))
                last.then_inc(s_lt, 1)

            def transpose_tile(i, j, first):
                t = i * TB + j
                pe.wait_ge(s_norm, t + 1)
                if not (first and j < RING):
                    pe.wait_ge(s_hT, t - RING + 1)
                for k in range(KC):
                    last = pe.transpose(ps_T[j % RING][:, k * P:(k + 1) * P], xg[:, j, k * P:(k + 1) * P], ident[:, :])
                last.then_inc(s_T, 1)

            def multiply(i, j, first, rel):
                t = i * TB + j
                pe.wait_ge(s_hT, t + 1)
                if not (first and j < RING):
                    pe.wait_ge(s_mg, t - RING + 1)
                for k in range(KC):
                    last = mm(ps_M[j % RING], hT[:, j % RING, k * P:(k + 1) * P],
                              W[:, bass.ds(rel * (KC * D) + k * D, D)], k == 0, k == KC - 1)
                last.then_inc(s_mm, 1)

            def scatter_windows(n, g, start=False):
                pe.wait_ge(s_rv, n + 1)
                if start:
                    any_row = OHW[:, 0, 0:2 * NW // LANES + 1, :].rearrange("p w c -> p (w c)")[:, 0:2 * NW]
                    mm(ps_win, zeros16[0:EP, :], any_row, True)
                for c in range(LANES):
                    for v in range(2):
                        last = mm(ps_win[:, v * NW:(v + 1) * NW], RV[g][:, v, :, c],
                                  OHW[:, bass.ds(n, 1), :, c].rearrange("p n w -> p (n w)"))
                last.then_inc(s_rvps, 1)

            def load_rel(i, g):
                packed = pe.value_load(rel_i[0:1, bass.ds(i * RING + g, 1)], min_val=0, max_val=RB ** LANES - 1)
                return [(packed // RB ** k) % RB for k in range(LANES)]

            def body(i, first, second=False):
                rel = [None] * LANES if first else load_rel(i - 1, RING - 1)
                for j in range(TB):
                    g = j // LANES
                    if j % LANES == 0:
                        rel += load_rel(i, g)
                    transpose_tile(i, j, first)
                    if j >= 2:
                        multiply(i, j - 2, first, rel[j - 2 + LANES])
                    elif not first:
                        multiply(i - 1, j - 2 + TB, False, rel[LANES - 2 + j])
                    if j % LANES == LANES - 1:
                        if not first:
                            scatter_windows((i - 1) * RING + g, g, second and g == 0)

            pe.wait_ge(s_w, 16)
            pe.wait_ge(s_list, 1)
            for k in range(RING):
                count_lanes(k)
            first_ranks()
            body(0, True)
            body(1, False, True)
            with pe.Fori(2, LAPS) as i:
                body(i, False)
            rel = load_rel(LAPS - 1, RING - 1)
            for j in range(TB - 2, TB):
                multiply(LAPS - 1, j, False, rel[j - TB])
            for g in range(RING):
                scatter_windows(NG - RING + g, g)
            pe.wait_ge(s_over, 1)
            mm(ps_over, ones16[0:EP, :], over16[:, :], True, True).then_inc(s_overps, 1)

            def sum_window(w, k, s, sel, rows, lap1):
                pw = ps_W[s]
                mm(pw[:, 0:2 * D], ones_b[:, :], bias3[:, :, :].rearrange("p a d -> p (a d)"), True)
                mm(pw[:, 2 * D:3 * D], ones_b[:, :], bias3[:, 0, :], True)
                pe.wait_ge(s_sel, w + 1)
                pe.wait_ge(s_wg[k], 16 * lap1)
                for b in range(BL):
                    last = mm(pw[:, b * D:(b + 1) * D], sel[:, b, :], rows)
                last.then_inc(s_wmm, 1)

            def windows(lap, first):
                for k in range(WB):
                    w = lap * WB + k
                    if not (first and k < 2):
                        pe.wait_ge(s_fin, w - 1)
                    sum_window(w, k, k % 2, S[:, k % SS], gm[:, k, :], lap + 1)

            pe.wait_ge(s_mg, MT)
            windows(0, True)
            with pe.Fori(1, XLAPS) as lap:
                windows(lap, False)
            pe.wait_ge(s_fin, NW - 2)
            sum_window(NW - 1, 0, 0, S[:, 0], gm[:, 0, :], XLAPS + 1)

            pe.wait_ge(s_win, 1)
            n_over = pe.value_load(over_i[0:1, 0:1], min_val=0, max_val=E)
            with pe.If(n_over > 0):
                def scatter_src(c, start):
                    pe.wait_ge(s_a_sc, c + 1)
                    mm(ps_dst, a_lane, a_tile[:, :], start).then_inc(s_a_ps, 1)

                scatter_src(0, True)
                with pe.Fori(1, EC) as c:
                    scatter_src(c, False)
                with pe.Fori(0, NW) as w:
                    pe.wait_ge(s_a_win, w + 1)
                    mm(ps_W[0][:, 0:2 * D], ones_b[:, :], bias3[:, :, :].rearrange("p a d -> p (a d)"), True)
                    mm(ps_W[0][:, 2 * D:3 * D], ones_b[:, :], bias3[:, 0, :], True)
                    with pe.Fori(0, LAPS) as q:
                        pe.wait_ge(s_a_msg, 16 * (w * LAPS + q + 1))
                        for j in range(TB):
                            pe.wait_ge(s_a_sel, (w * LAPS + q) * TB + j + 1)
                            for b in range(BL):
                                last = mm(ps_W[0][:, b * D:(b + 1) * D], S[:, j % SS, b, :], xg[:, j, :])
                            last.then_inc(s_a_mm, 1)

        @block.vector
        def _(dve):
            v = nc.vector
            c = Count(dve, s_dve)

            def ts(o, a, s1, op0, s2=None, op1=None):
                if op1 is None:
                    return v.tensor_scalar(o, a, s1, None, op0)
                return v.tensor_scalar(o, a, s1, s2, op0, op1)

            def stt(o, a, s1, op0, b, op1):
                return v.scalar_tensor_tensor(out=o, in0=a, scalar=s1, in1=b, op0=op0, op1=op1)

            def tt(o, a, b, op):
                return v.tensor_tensor(o, a, b, op)

            def of_group(a, n, count):
                return a[:, bass.ds(n, 1), 0:LANES].to_broadcast([EP, count, LANES])

            def one_hot(o, a, n, count):
                return tt(o, iota_c[0:EP, 0:count, :], of_group(a, n, count), ALU.is_equal)

            def columns(a):
                return a[:, 0:EC // LANES, 0:LANES]

            def by_group(a):
                return a.rearrange("p (n c) -> p n c", c=LANES)

            v.memset(eps[:], EPS).then_inc(s_const, 1)
            for t, value in ((ones16, 1.0), (zeros16, 0.0), (ones_b, 1.0), (xt, 0.0), (tiles, 0.0)):
                c.up(v.memset(t[:], value))
            c.up(v.memset(cols[:, 0:3, :, :], -1.0))
            c.up(v.memset(cols[:, 3:7, :, :], 0.0))
            for t in scan:
                c.up(v.memset(t[:, :, 0:PADC], 0.0))
            dve.wait_ge(s_iota, 3)
            c.up(v.tensor_copy(iota_c[:, :, :], iota16[:, :, None].to_broadcast([P, iota_n, LANES])))
            c.up(ts(ident[:, :], iota16[:, 0:P], part[:, 0:1], ALU.is_equal))
            c.up(ts(ident16[:, :], iota16[:, 0:P], part[:, 0:1], ALU.is_equal))
            done = c.up(ts(before16[:, :], iota16[:, 0:P], part[:, 0:1], ALU.is_gt))

            dve.wait_ge(s_edge, 48)
            c.wait(done)
            c.chain(v.tensor_copy(typ16[:, :], typ_i[:, :]))
            c.chain(tt(scan[2][:, :, PADC:], typ16[:, None, :].to_broadcast([EP, R, EC]),
                       iota16[0:EP, 0:R, None].to_broadcast([EP, R, EC]), ALU.is_equal))
            frm, to, step = scan[2], scan[0], 1
            while step < EC:
                assert step <= PADC
                ins = tt(to[:, :, PADC:], frm[:, :, PADC:], frm[:, :, PADC - step:PADC - step + EC], ALU.add)
                step *= 2
                if step >= EC:
                    ins.then_inc(s_tot, 1)
                    assert to is scan[0]
                else:
                    c.chain(ins)
                    frm, to = to, scan[1] if to is scan[0] else scan[0]

            dve.wait_ge(s_relps, 1)
            c.chain(ts(cnt_i[:, 0, :], ps_cnt, float(P - 1), ALU.add))
            c.chain(ts(cnt_i[:, 1, :], cnt_i[:, 0, :], P.bit_length() - 1, ALU.arith_shift_right))
            c.chain(v.tensor_copy(tiles[:, 0, R:], cnt_i[:, 1, :]))
            frm, to, step = 0, 1, 1
            while step < R:
                c.chain(tt(tiles[:, to, R:], tiles[:, frm, R:], tiles[:, frm, R - step:2 * R - step], ALU.add))
                frm, to, step = to, frm, 2 * step
            first_tile = tiles[:, frm, R - 1:2 * R - 1]
            c.chain(stt(base[:, :], first_tile[0:EP, :], float(P), ALU.mult, ps_rel, ALU.add))
            dve.wait_ge(s_tot, 1)
            c.chain(tt(sc_sum[:, :, :], scan[0][:, :, PADC:], base[:, :, None].to_broadcast([EP, R, EC]), ALU.add))
            c.chain(tt(sc_sel[:, :, :], sc_sum[:, :, :], scan[2][:, :, PADC:], ALU.mult))
            c.chain(v.tensor_reduce(pos[:, :], sc_sel[:, :, :].rearrange("p r c -> p c r"), AX_X, ALU.add))
            c.chain(ts(pos_i[:, :], pos[:, :], -1.0, ALU.add))
            c.up(ts(tmp_i[:, 0, :], pos_i[:, :], P - 1, ALU.bitwise_and))
            c.up(ts(tmp_i[:, 1, :], pos_i[:, :], P.bit_length() - 1, ALU.arith_shift_right))
            c.up(ts(tmp_i[:, 2, :], dst_i[:, :], 8, ALU.arith_shift_right))
            c.chain(ts(tmp_i[:, 3, :], dst_i[:, :], 255, ALU.bitwise_and))
            for k, t in enumerate((lane16, tile16, dhi16, dlo16)):
                done = c.up(v.tensor_copy(columns(t), by_group(tmp_i[:, k, :])))
            c.wait(done)

            def scatter_dst(i, g, first):
                n = i * RING + g
                if not first:
                    dve.wait_ge(s_scps, n - RING + 1)
                c.up(one_hot(OHL[g], lane16, n, P))
                c.chain(one_hot(OHT[g][:, 0:MT, :], tile16, n, MT))
                c.up(tt(HV[g][:, 0:MT, :], OHT[g][:, 0:MT, :], of_group(dhi16, n, MT), ALU.mult))
                tt(HV[g][:, MT:, :], OHT[g][:, 0:MT, :], of_group(dlo16, n, MT), ALU.mult).then_inc(s_sc, 1)

            for g in range(RING):
                scatter_dst(0, g, True)
            with dve.Fori(1, LAPS) as i:
                c.loop(i - 1, 3 * RING)
                for g in range(RING):
                    scatter_dst(i, g, False)
            c.end(LAPS - 1)

            c.chain(tt(rel_ge[:, :, :], iota16[0:1, 0:MT, None].to_broadcast([1, MT, R]),
                       first_tile[0:1, None, :].to_broadcast([1, MT, R]), ALU.is_ge))
            c.chain(v.tensor_reduce(rel_f[:, :], rel_ge[:, :, :], AX_X, ALU.add))
            c.chain(ts(rel_f[:, :], rel_f[:, :], -1.0, ALU.add))
            digits = rel_f[:, :].rearrange("p (n k) -> p k n", k=LANES)
            acc = digits[:, LANES - 1, :]
            for k in reversed(range(1, LANES - 1)):
                c.chain(stt(rel_p[:, k, :], acc, float(RB), ALU.mult, digits[:, k, :], ALU.add))
                acc = rel_p[:, k, :]
            done = c.up(stt(rel_i[:, :], acc, float(RB), ALU.mult, digits[:, 0, :], ALU.add))
            dve.wait_ge(s_scps, NG)
            c.chain(v.tensor_copy(dlo_f[:, :], ps_dst[:, MT:2 * MT]))
            c.wait(done)
            stt(dst_list[:, :], ps_dst[:, 0:MT], 256.0, ALU.mult, dlo_f[:, :], ALU.add).then_inc(s_list, 1)

            c.chain(ts(tmp_i[:, 4, :], src_i[:, :], 7, ALU.arith_shift_right))
            c.chain(ts(tmp_i[:, 5, :], tmp_i[:, 4, :], float(DIV), ALU.mult))
            c.chain(ts(tmp_i[:, 6, :], tmp_i[:, 5, :], 9, ALU.arith_shift_right))
            c.chain(v.tensor_copy(columns(win16), by_group(tmp_i[:, 6, :])))
            third = NG // RING

            def window_hots(k):
                ws = slice(k * third, (k + 1) * third)
                tt(OHW[:, ws, :, :], iota_c[0:EP, None, 0:NW, :].to_broadcast([EP, third, NW, LANES]),
                   win16[:, ws, None, 0:LANES].to_broadcast([EP, third, NW, LANES]), ALU.is_equal).then_inc(s_ohw, 1)

            def group(i, g, tiles_too=True, columns_too=True, rv_used=True):
                n = i * RING + g
                m = n - RING
                if tiles_too:
                    dve.wait_ge(s_gather[g], 16 * LANES * (i + 1))
                    for k in range(LANES):
                        c.up(v.bn_stats(stats[:, g, k, :], xg[:, g * LANES + k, :]))
                if columns_too:
                    ohw = OHW[:, bass.ds(m, 1), :, :].rearrange("p n w c -> p (n w) c")
                    c.chain(tt(prod[:, :, :], ohw, C[:, :, :], ALU.mult))
                    with nc.allow_low_precision(reason="one term is not zero; whole numbers, exact up to 2048"):
                        rank = c.up(v.tensor_reduce(rank16[:, bass.ds(m, 1), 0:LANES].rearrange("p n c -> p (n c)"),
                                                    prod[:, :, :].rearrange("p w c -> p c w"), AX_X, ALU.add))
                else:
                    c.wait(c.base + c.n)
                if tiles_too:
                    for k in range(LANES):
                        v.bn_aggr(mv[:, g, k, :], stats[:, g, k, :]).then_inc(s_var, 1)
                if columns_too:
                    c.up(tt(C[:, :, :], C[:, :, :], ohw, ALU.add))
                    c.wait(rank)
                    if rv_used:
                        dve.wait_ge(s_rvps, m - RING + 1)
                    c.chain(one_hot(OHR[g], rank16, m, P))
                    c.up(tt(RV[g][:, 0, :, :], OHR[g], of_group(v1, m, P), ALU.mult))
                    tt(RV[g][:, 1, :, :], OHR[g], of_group(v2, m, P), ALU.mult).then_inc(s_rv, 1)
                if tiles_too:
                    dve.wait_ge(s_std, n + 1)
                    c.chain(v.reciprocal(rstd[:, g, :], std[:, g, :]))
                    stt(nmr[:, g, :], mv[:, g, :, 0], -1.0, ALU.mult, rstd[:, g, :], ALU.mult).then_inc(s_ln, 1)

            for k in range(RING):
                window_hots(k)
            dve.wait_ge(s_bias, 48)
            c.chain(v.tensor_copy(bias_part[:, 0, :], bias_row))
            c.chain(tt(bias_rest[:, 0, :], bias_row, bias_part[:, 0, :], ALU.subtract))
            c.chain(v.tensor_copy(bias_part[:, 1, :], bias_rest[:, 0, :]))
            c.chain(tt(bias_rest[:, 1, :], bias_rest[:, 0, :], bias_part[:, 1, :], ALU.subtract))
            c.chain(v.tensor_copy(bias_part[:, 2, :], bias_rest[:, 1, :]))
            c.chain(ts(bias_sel[:, 0, :], bias_part[:, 0, :], ident[0:3, 0:1], ALU.mult))
            c.chain(stt(bias_sel[:, 1, :], bias_part[:, 1, :], ident[0:3, 1:2], ALU.mult, bias_sel[:, 0, :], ALU.add))
            for k in range(2):
                c.up(stt(bias3[:, k, :], bias_part[:, 2, :], ident[0:3, 2:3], ALU.mult, bias_sel[:, 1, :], ALU.add))
            group(0, 0, columns_too=False)
            dve.wait_ge(s_lt, 1)
            c.chain(v.tensor_copy(LT[:, ps_L[0][1], :], ps_L[0][0]))
            v.tensor_copy(LT[:, ps_L[1][1], :], ps_L[1][0]).then_inc(s_ohw, 1)
            group(0, 1, columns_too=False)
            dve.wait_ge(s_lt, 2)
            for o, ws in ps_L:
                done = c.up(v.tensor_copy(C[:, ws, :], o))
            c.chain(stt(srel[:, :], tmp_i[:, 6, :], float(-WIN), ALU.mult, src_i[:, :], ALU.add))
            c.up(ts(tmp_i[:, 7, :], pos_i[:, :], 7, ALU.bitwise_and))
            c.chain(ts(tmp_i[:, 4, :], pos_i[:, :], 3, ALU.arith_shift_right))
            c.up(ts(columns(v1), by_group(tmp_i[:, 4, :]), 16.0, ALU.add))
            c.chain(stt(v2f[:, :], tmp_i[:, 7, :], 512.0, ALU.mult, srel[:, :], ALU.add))
            c.chain(ts(columns(v2), by_group(v2f[:, :]), -2048.0, ALU.add))
            group(0, 2, columns_too=False)
            for g in range(RING):
                group(1, g, rv_used=False)
            PER = RING * (LANES + 6)
            with dve.Fori(2, LAPS) as i:
                c.loop(i - 2, PER)
                for g in range(RING):
                    group(i, g)
            c.end(LAPS - 2)
            for g in range(RING):
                group(LAPS, g, tiles_too=False)

            c.chain(ts(over[:, :, 0:LANES], rank16[:, :, 0:LANES], float(P), ALU.is_ge))
            c.chain(v.tensor_reduce(over_n[:, :], over[:, :, 0:LANES], mybir.AxisListType.XY, ALU.add))
            v.tensor_copy(over16[:, :], over_n[:, :]).then_inc(s_over, 1)
            dve.wait_ge(s_overps, 1)
            c.up(v.tensor_copy(over_i[:, :], ps_over))
            dve.wait_ge(s_rvps, NG)
            empty, row = li_f[:, 6, :], li_f[:, 1, :]
            c.chain(v.tensor_copy(li[:, 0, :], ps_win[:, 0:NW]))
            c.up(ts(li[:, 1, :], ps_win[:, NW:2 * NW], 2048.0, ALU.add))
            c.chain(ts(empty, ps_win[:, 0:NW], 0.5, ALU.is_lt))
            c.up(ts(li[:, 2, :], li[:, 0, :], 4, ALU.arith_shift_right))
            c.up(ts(li[:, 3, :], li[:, 0, :], 15, ALU.bitwise_and))
            c.up(ts(li[:, 4, :], li[:, 1, :], 9, ALU.arith_shift_right))
            c.chain(ts(li[:, 5, :], li[:, 1, :], 511, ALU.bitwise_and))
            c.up(stt(src_list[:, :], empty, -1024.0, ALU.mult, li[:, 5, :], ALU.add))
            c.chain(stt(row, li[:, 3, :], 8.0, ALU.mult, li[:, 4, :], ALU.add))
            c.chain(stt(row, row, float(MT), ALU.mult, li[:, 2, :], ALU.add))
            c.chain(ts(row, row, -1.0, ALU.add))
            stt(row_list[:, :], empty, float(NONE), ALU.mult, row, ALU.add).then_inc(s_win, 1)
            dve.wait_ge(s_win, 1)

            def select(lap, k, first):
                w = lap * WB + k
                if not (first and k < SS):
                    dve.wait_ge(s_wmm, w - SS + 1)
                ts(S[:, k % SS], iota_node[:, :, :], src_list[:, bass.ds(w, 1)], ALU.is_equal).then_inc(s_sel, 1)

            def finish(lap, k):
                w = lap * WB + k
                dve.wait_ge(s_wmm, w + 1)
                if k % GW == 0:
                    dve.wait_ge(s_x[k // GW], 16 * (lap + 1))
                xs = xr[:, bass.ds(x_slot(lap, 0) + k, 1), :].rearrange("p w n -> p (w n)")
                stt(xs, ps_W[k % 2], 0.0, ALU.max, xs, ALU.add).then_inc(s_fin, 1)

            def windows(lap, first):
                for k in range(2):
                    select(lap, k, first)
                for k in range(WB):
                    finish(lap, k)
                    if k + 2 < WB:
                        select(lap, k + 2, first)

            windows(0, True)
            with dve.Fori(1, XLAPS) as lap:
                windows(lap, False)
            select(XLAPS, 0, False)
            dve.wait_ge(s_wmm, NW)
            dve.wait_ge(s_tail, 32)
            stt(xt[:, :], ps_W[0][0:TAILP, :], 0.0, ALU.max, xt[:, :], ALU.add).then_inc(s_fin, 1)

            n_over = dve.value_load(over_i[0:1, 0:1], min_val=0, max_val=E)
            with dve.If(n_over > 0):
                dve.wait_ge(s_fin, NW)
                c.up(ts(tmp_i[:, 0, :], src_i[:, :], 8, ALU.arith_shift_right))
                c.chain(ts(tmp_i[:, 1, :], src_i[:, :], 255, ALU.bitwise_and))
                c.up(ts(a_val[:, 0, :], tmp_i[:, 0, :], 1.0, ALU.add))
                c.chain(v.tensor_copy(a_val[:, 1, :], tmp_i[:, 1, :]))
                c.up(v.tensor_copy(by_group(a_pos[:, 0, :]), columns(lane16)))
                c.chain(v.tensor_copy(by_group(a_pos[:, 1, :]), columns(tile16)))

                def scatter_src(col, first):
                    one = bass.ds(col, 1)
                    if not first:
                        dve.wait_ge(s_a_ps, col)
                    c.up(ts(a_lane, iota16[0:EP, 0:P], a_pos[:, 0, one], ALU.is_equal))
                    c.chain(ts(a_tile[:, 0:MT], iota16[0:EP, 0:MT], a_pos[:, 1, one], ALU.is_equal,
                               a_val[:, 0, one], ALU.mult))
                    ts(a_tile[:, MT:2 * MT], iota16[0:EP, 0:MT], a_pos[:, 1, one], ALU.is_equal,
                       a_val[:, 1, one], ALU.mult).then_inc(s_a_sc, 1)

                scatter_src(0, True)
                with dve.Fori(1, EC) as col:
                    c.loop(col - 1, 2)
                    scatter_src(col, False)
                c.end(EC - 1)
                dve.wait_ge(s_a_ps, EC)
                c.chain(ts(dlo_f[:, :], ps_dst[:, MT:2 * MT], -256.0, ALU.add))
                c.chain(stt(src_slot[:, :], ps_dst[:, 0:MT], 256.0, ALU.mult, dlo_f[:, :], ALU.add))
                v.memset(over[:, 0, :], 0.0).then_inc(s_a_mm, SS)
                v.memset(over16[:, :], 0.0).then_inc(s_a_win, 1)

                def window(w, parts, done_x):
                    with dve.Fori(0, LAPS) as q:
                        for j in range(TB):
                            dve.wait_ge(s_a_mm, (w * LAPS + q) * TB + j + 1)
                            ts(S[:, j % SS], iota_node[:, :, :], src_slot[:, bass.ds(q * TB + j, 1)],
                               ALU.is_equal).then_inc(s_a_sel, 1)
                    dve.wait_ge(s_a_mm, SS + (w + 1) * MT)
                    c.chain(ts(src_slot[:, :], src_slot[:, :], float(-WIN), ALU.add))
                    dve.wait_ge(s_a_x, done_x)
                    stt(xr[0:parts, 0, :], ps_W[0][0:parts, :], 0.0, ALU.max, xr[0:parts, 0, :],
                        ALU.add).then_inc(s_a_win, 1)

                with dve.Fori(0, NW - 1) as w:
                    c.loop(w, 1)
                    window(w, P, 16 * (w + 1))
                c.end(NW - 1)
                window(NW - 1, TAILP, 16 * (NW + 1))


_INS = ["x", "src", "dst", "edge_type_8", "L0_gnn_weight", "L0_gnn_bias"]


def kernel(**inputs):
    import numpy as _np
    import concourse.bacc as _bacc
    from concourse import mybir as _mybir
    from concourse.bass_utils import run_bass_kernel_spmd as _run

    nc = _bacc.Bacc("TRN2", target_bir_lowering=False, num_devices=1)
    arrays, args = {}, []
    for name in _INS:
        a = _np.ascontiguousarray(inputs[name])
        arrays[f"in_{name}"] = a
        args.append(nc.dram_tensor(f"in_{name}", a.shape, _mybir.dt.from_np(a.dtype), kind="ExternalInput").ap())
    shape = arrays["in_x"].shape
    args.append(nc.dram_tensor("out_0", shape, _mybir.dt.float32, kind="ExternalOutput").ap())
    gnn_kernel(nc, *args)
    r = _run(nc, [arrays], core_ids=[0])
    return r.results[0]["out_0"]
```

```python
from contextlib import ExitStack

import concourse.bass as bass
from concourse import mybir
from concourse.alu_op_type import AluOpType as ALU

P = 128
ACT = mybir.ActivationFunctionType
AX_X = mybir.AxisListType.X
F32 = mybir.dt.float32
F16 = mybir.dt.float16
BF16 = mybir.dt.bfloat16
I32 = mybir.dt.int32
EPS = 1e-5


class Count:

    def __init__(self, eng, sem):
        self.eng, self.sem, self.base, self.n, self.per, self.saved = eng, sem, 0, 0, 0, 0

    def up(self, ins):
        ins.then_inc(self.sem, 1)
        self.n += 1
        return self.base + self.n

    def wait(self, value):
        self.eng.wait_ge(self.sem, value)

    def chain(self, ins):
        self.wait(self.up(ins))

    def loop(self, i, per):
        self.saved, self.per = self.n, per
        self.base, self.n = i * per + self.n, 0

    def end(self, trips):
        assert self.n == self.per, (self.n, self.per)
        self.base, self.n = 0, self.saved + trips * self.per


def gnn_kernel(nc, x, src, dst, edge_type, weight, bias, out):
    NODES, D = x.shape
    E = src.shape[0]
    R = weight.shape[0]
    KC = D // P
    EP = max(p for p in range(1, P + 1) if E % p == 0)
    EC = E // EP
    MT = (E - R) // P + R
    LANES = 5
    RING = 3
    NG = MT // LANES
    LAPS = NG // RING
    ECP = NG * LANES
    TB = LANES * RING
    assert MT == NG * LANES and NG == LAPS * RING and EC <= ECP and EP <= P
    BL = 3
    WIN = BL * P
    NW = -(-NODES // WIN)
    GW = 2
    XK = 5
    WB = GW * XK
    XLAPS = (NW - 1) // WB
    XRING = 3
    TAIL = NODES - (NW - 1) * WIN
    TAILP = -(-TAIL // BL)
    TAILF = TAIL // BL
    assert NW - 1 == XLAPS * WB and 0 < TAIL < WIN and XLAPS > XRING
    EL = XRING
    NE = EL * WB
    MAIN = XLAPS - EL
    FX = XK
    FL = NE // FX
    assert LAPS == 1 + 2 * XRING and XK < 2 * RING
    assert NE == FX * FL and 2 <= FL <= MAIN - 3 and GW == 2 and FX + WB <= TB
    assert TAILP > TAILF
    ROWS = MT * P
    NONE = 1 << 17
    assert ROWS // 8 + 16 <= 2048 and WIN <= 512 and NODES < 1 << 16
    RB = 8
    assert R <= RB
    DIV = 171
    assert BL == 3 and NODES >> 7 < 512
    W0 = 512 // LANES
    GC = LANES + LANES % 2

    msg = nc.dram_tensor("messages", (ROWS, D), F32, kind="Internal").ap()
    msg_by_lane = msg.rearrange("(p t) d -> p t d", t=MT)

    with ExitStack() as ctx:
        def sb(name, shape, dt):
            return ctx.enter_context(nc.sbuf_tensor(name, shape, dt))

        def sem(name):
            return ctx.enter_context(nc.semaphore(name))

        iota_n = max(P, MT, NW)
        iota16 = sb("iota16", [P, iota_n], F16)
        iota_c = sb("iota_c", [P, iota_n, LANES], F16)
        iota_node = sb("iota_node", [P, BL, P], F32)
        part = sb("part", [P, 1], F32)
        ident = sb("ident", [P, P], F32)
        ident16 = sb("ident16", [P, P], F16)
        before16 = sb("before16", [P, P], F16)
        ones16 = sb("ones16", [P, P], F16)
        eps = sb("eps", [P, 1], F32)
        sqrt_eps = sb("sqrt_eps", [P, 1], F32)
        zeros16 = sb("zeros16", [P, P], F16)
        ones_b = sb("ones_b", [3, P], BF16)
        bias3 = sb("bias3", [3, 2, D], BF16)
        brelu = sb("brelu", [P, D], F32)
        W = sb("W", [P, R * KC * D], F32)

        typ_i = sb("typ_i", [EP, EC], I32)
        dst_i = sb("dst_i", [EP, EC], I32)
        src_i = sb("src_i", [EP, EC], I32)
        typ16 = sb("typ16", [EP, EC], F16)
        tmp_i = sb("tmp_i", [EP, 8, EC], I32)
        pos = sb("pos", [EP, EC], F32)
        pos_i = sb("pos_i", [EP, EC], I32)
        srel = sb("srel", [EP, EC], F32)
        v2f = sb("v2f", [EP, EC], F32)
        cols = sb("cols", [EP, 7, NG, GC], F16)
        lane16, tile16, win16, dhi16, dlo16, v1, v2 = (cols[:, k, :, :] for k in range(7))
        rank16 = sb("rank16", [EP, NG, GC], F16)
        over = sb("over", [EP, NG, GC], F16)
        over_n = sb("over_n", [EP, 1], F32)
        over16 = sb("over16", [EP, 1], F16)
        over_i = sb("over_i", [P, 1], I32)
        base = sb("base", [EP, R], F32)
        cnt_i = sb("cnt_i", [P, 2, R], I32)
        tiles = sb("tiles", [P, 2, 2 * R], F32)
        rel_ge = sb("rel_ge", [1, MT, R], F32)
        MLAG = 2
        assert MLAG < LANES
        rel_f = sb("rel_f", [1, (NG + 1) * LANES], F32)
        rel_p = sb("rel_p", [1, LANES, NG + 1], F32)
        rel_i = sb("rel_i", [1, NG + 1], I32)
        dlo_f = sb("dlo_f", [P, MT], F32)
        dst_list = sb("dst_list", [P, MT], I32)
        OHW = sb("OHW", [EP, NG, NW, LANES], F16)
        LT = sb("LT", [EP, NW, LANES], F16)
        C = sb("C", [EP, NW, LANES], F16)
        prod = sb("prod", [EP, NW, LANES], F16)
        RW = RING * 3 * P * LANES // 2
        ranks = sb("ranks", [P, RW], F32)
        RV = [ranks[0:EP, g * P * LANES:(g + 1) * P * LANES].bitcast(F16)
              .rearrange("p (v r c) -> p v r c", v=2, c=LANES) for g in range(RING)]
        OHR = [ranks[0:EP, (2 * RING + g) * P * LANES // 2:(2 * RING + g + 1) * P * LANES // 2].bitcast(F16)
               .rearrange("p (r c) -> p r c", c=LANES) for g in range(RING)]

        row_list = sb("row_list", [P, NW], I32)
        src_list = sb("src_list", [P, NW], F32)

        fix_list = sb("fix_list", [P, NE, 2], I32)

        xg = sb("xg", [P, TB, D], F32)
        mg = sb("mg", [P, TB, D], F32)
        hT = sb("hT", [P, RING, KC * P], F32)
        stage1 = sb("stage1", [P, RING, LANES], I32)
        stats = sb("stats", [P, RING, LANES, 6], F32)
        mv = sb("mv", [P, RING, LANES, 2], F32)
        std = sb("std", [P, RING, LANES], F32)
        rstd = sb("rstd", [P, RING, LANES], F32)
        nmr = sb("nmr", [P, RING, LANES], F32)

        PADC = 64
        mg_flat = mg[:, :, :].rearrange("p t d -> p (t d)")
        xg_flat = xg[:, :, :].rearrange("p t d -> p (t d)")
        sc_sum, sc_sel = (mg_flat[0:EP, k * R * EC:(k + 1) * R * EC].rearrange("p (r c) -> p r c", r=R)
                          for k in range(2))
        scan_w = R * (PADC + EC) // 2
        at = 2 * R * EC
        scan = [mg_flat[0:EP, at + k * scan_w:at + (k + 1) * scan_w].bitcast(F16)
                .rearrange("p (r c) -> p r c", r=R) for k in range(3)]
        assert at + 3 * scan_w <= TB * D
        at = 0
        OHL, OHT, HV = [], [], []
        for g in range(RING):
            for lst, n in ((OHL, P), (OHT, MT + 1), (HV, 2 * MT)):
                w = LANES * n // 2
                lst.append(xg_flat[0:EP, at:at + w].bitcast(F16).rearrange("p (n c) -> p n c", c=LANES))
                at += w
        assert at <= TB * D
        gm = xg
        SS = 5
        S = ranks[:, 0:SS * WIN].rearrange("p (s b n) -> p s b n", s=SS, b=BL)
        li_f = ranks[:, SS * WIN:SS * WIN + 7 * NW].rearrange("p (k w) -> p k w", w=NW)
        li = li_f.bitcast(I32)
        assert WB <= TB and SS * WIN + 7 * NW <= RW
        stage3 = sb("stage3", [P, XK, GW], I32)
        fm = [gm[:, WB + k, :] for k in range(FX)]
        xf = [mg[:, k, :] for k in range(FX)]
        fd = [mg[:, FX + k, 0:P // 2].bitcast(F16) for k in range(FX)]
        fq = [mg[:, 2 * FX + k, 0:P] for k in range(FX)]
        stage4 = sb("stage4", [P, FX, 2], I32)
        XS = XRING * XK
        xr = sb("xr", [P, XS * GW, BL * D], F32)
        xt = sb("xt", [TAILP, BL * D], F32)

        bias_row = xt[0:3, 0:D]
        bias_rest = xt[0:3, D:3 * D].rearrange("p (k d) -> p k d", d=D)
        bias_part, bias_sel = (mg_flat[0:3, a * D:a * D + n * D // 2].bitcast(BF16).rearrange("p (k d) -> p k d", d=D)
                               for a, n in ((TB - 3, 3), (TB - 1, 2)))

        a_val, a_pos = (mg[0:EP, k, 0:2 * EC].rearrange("p (k c) -> p k c", k=2) for k in range(2))
        a_lane = OHR[0].rearrange("p r c -> p (r c)")[:, 0:P]
        a_tile = OHW[:, 0, :, :].rearrange("p w c -> p (w c)")[:, 0:2 * MT]
        src_slot = mg[:, 2, 0:MT]

        ps = ctx.enter_context(nc.psum_tensor("ps", [P, 8 * 512], F32))

        def bank(b, a, z, parts=P):
            return ps[0:parts, 512 * b + a:512 * b + z]

        ps_T = [bank(b, 0, KC * P) for b in (0, 1, 4)]
        ps_M = [bank(b, 0, D) for b in (2, 3, 5)]
        ps_L = [(bank(6, 0, W0 * LANES, EP).rearrange("p (w l) -> p w l", l=LANES), slice(0, W0)),
                (bank(7, 0, (NW - W0) * LANES, EP).rearrange("p (w l) -> p w l", l=LANES), slice(W0, NW))]
        ps_dst = bank(6, 0, 2 * MT)
        ps_over = bank(6, 0, 1)
        ps_rel = bank(7, 0, R, EP)
        ps_cnt = bank(7, R, 2 * R)
        ps_win = bank(7, 0, 2 * NW)
        ps_W = [ps[:, 1024 * k:1024 * k + BL * D] for k in range(2)]
        ps_row = bank(4, 0, P)
        ps_fix = [bank(5 + k % 3, 0, D) for k in range(FX)]
        assert (NW - W0) * LANES <= 512 and 2 * MT <= 512 and BL * D <= 1024

        s_edge = sem("s_edge")
        s_bias = sem("s_bias")
        s_w = sem("s_w")
        s_bias3 = sem("s_bias3")
        s_tail = sem("s_tail")
        s_brelu = sem("s_brelu")
        s_relu = sem("s_relu")
        s_early = sem("s_early")
        s_iota = sem("s_iota")
        s_dve = sem("s_dve")
        s_const = sem("s_const")
        s_tot = sem("s_tot")
        s_relps = sem("s_relps")
        s_sc = sem("s_sc")
        s_scps = sem("s_scps")
        s_dstps = sem("s_dstps")
        s_list = sem("s_list")
        s_ohw = sem("s_ohw")
        s_lt = sem("s_lt")
        s_stage = sem("s_stage")
        s_lists = sem("s_lists")
        s_gather = [sem(f"s_gather{g}") for g in range(RING)]
        s_var = sem("s_var")
        s_std = sem("s_std")
        s_ln = sem("s_ln")
        s_norm = sem("s_norm")
        s_T = sem("s_T")
        s_hT = sem("s_hT")
        s_mm = sem("s_mm")
        s_mg = sem("s_mg")
        s_mst = [sem(f"s_mst{g}") for g in range(RING)]
        s_rv = sem("s_rv")
        s_rvps = sem("s_rvps")
        s_held = sem("s_held")
        s_win = sem("s_win")
        s_overps = sem("s_overps")
        s_over = sem("s_over")
        s_wg = [sem(f"s_wg{k}") for k in range(WB)]
        s_sel = sem("s_sel")
        s_wmm = sem("s_wmm")
        s_fin = sem("s_fin")
        s_x = [sem(f"s_x{k}") for k in range(XK)]
        s_out = [sem(f"s_out{k}") for k in range(XK)]
        s_outt = sem("s_outt")
        s_fg = [sem(f"s_fg{k}") for k in range(FX)]
        s_fd = sem("s_fd")
        s_frow = sem("s_frow")
        s_fq = sem("s_fq")
        s_fsum = sem("s_fsum")
        s_ff = sem("s_ff")
        s_fs = [sem(f"s_fs{k}") for k in range(FX)]
        s_a_sc = sem("s_a_sc")
        s_a_ps = sem("s_a_ps")
        s_a_list = sem("s_a_list")
        s_a_msg = sem("s_a_msg")
        s_a_sel = sem("s_a_sel")
        s_a_mm = sem("s_a_mm")
        s_a_win = sem("s_a_win")
        s_a_x = sem("s_a_x")
        s_a_out = sem("s_a_out")

        x_groups = x[0:XLAPS * WB * WIN, :].rearrange("(g w p b) d -> g p w (b d)", w=GW, p=P, b=BL)
        out_groups = out[0:XLAPS * WB * WIN, :].rearrange("(g w p b) d -> g p w (b d)", w=GW, p=P, b=BL)
        x_wins = x[0:XLAPS * WB * WIN, :].rearrange("(w p b) d -> w p (b d)", p=P, b=BL)
        out_wins = out[0:XLAPS * WB * WIN, :].rearrange("(w p b) d -> w p (b d)", p=P, b=BL)
        t0 = (NW - 1) * WIN
        tail_full = slice(t0, t0 + TAILF * BL)
        tail_rest = slice(t0 + TAILF * BL, NODES)
        REST = NODES - tail_rest.start

        def tail_dma(eng, dram, tile, load, done):
            full = dram[tail_full, :].rearrange("(p b) d -> p (b d)", b=BL)
            rest = dram[tail_rest, :].rearrange("(p b) d -> p (b d)", b=REST)
            for d, s in ((full, tile[0:TAILF, :]), (rest, tile[TAILF:TAILP, 0:REST * D])):
                eng.dma_start(*((s, d) if load else (d, s))).then_inc(done, 16)

        def x_slot(lap, k):
            return (lap % XRING) * WB + k * GW

        STAGED = ("w0", "w1", "f0", "w2", "f1", "w3", "f2", "w4", "f3", "f4")

        block = ctx.enter_context(nc.Block())

        @block.sync
        def _(sp):
            for t, d in ((typ_i, edge_type), (dst_i, dst), (src_i, src)):
                sp.dma_start(t[:, :], d.rearrange("(p c) -> p c", c=EC)).then_inc(s_edge, 16)

            def load_x(lap, k):
                if not (isinstance(lap, int) and lap == 0):
                    sp.wait_ge(s_x[k], 16 * lap)
                sp.dma_start(xr[:, bass.ds(x_slot(lap, k), GW), :],
                             x_groups[bass.ds(lap * XK + k, 1)].rearrange("g p w n -> p (g w) n")
                             ).then_inc(s_x[k], 16)

            def reload_x(lap, k):
                sp.wait_ge(s_out[k], 16 * (lap - XRING + 1))
                sp.sem_inc(s_held)
                load_x(lap, k)

            for k in range(XK):
                load_x(0, k)
            with sp.Fori(1, XRING) as lap:
                for k in range(XK):
                    load_x(lap, k)
            sp.dma_start(W[:, :].rearrange("p (r d) -> p r d", d=D),
                         weight.rearrange("r (k p) d -> p (r k) d", p=P)).then_inc(s_w, 16)
            sp.wait_ge(s_tot, 1)
            sp.dma_start(bias_row, bias.rearrange("(a d) -> a d", a=1).to_broadcast([3, D])).then_inc(s_bias, 16)

            def store_messages(i, g):
                sp.wait_ge(s_mg, (i * RING + g) * LANES + LANES)
                sp.dma_start(msg_by_lane[:, bass.ds((i * RING + g) * LANES, LANES), :],
                             mg[:, g * LANES:(g + 1) * LANES, :]).then_inc(s_mst[g], 16)

            for g in range(RING):
                store_messages(0, g)
            with sp.Fori(0, XRING) as pair:
                for q in range(2 * RING):
                    store_messages(1 + pair * 2 + q // RING, q % RING)
                    if q < XK:
                        reload_x(pair + XRING, q)

            sp.wait_ge(s_bias3, 2)
            tail_dma(sp, x, xt, True, s_tail)
            with sp.Fori(2 * XRING, XLAPS) as lap:
                for k in range(XK):
                    reload_x(lap, k)

            sp.wait_ge(s_win, 1)
            n_over = sp.value_load(over_i[0:1, 0:1], min_val=0, max_val=E)
            with sp.If(n_over > 0):
                sp.wait_ge(s_wmm, NW - NE)
                sp.wait_ge(s_fsum, NE)
                with sp.Fori(0, NW) as w:
                    with sp.Fori(0, LAPS) as q:
                        sp.wait_ge(s_a_mm, SS + (w * LAPS + q) * TB)
                        sp.dma_start(xg[:, :, :], msg_by_lane[:, bass.ds(q * TB, TB), :]).then_inc(s_a_msg, 16)

        @block.gpsimd
        def _(pool):
            pool.iota(iota16[:, :], [[1, iota_n]], base=0, channel_multiplier=0,
                      allow_small_or_imprecise_dtypes=True).then_inc(s_iota, 1)
            pool.iota(part[:, :], [[1, 1]], base=0, channel_multiplier=1,
                      allow_small_or_imprecise_dtypes=True).then_inc(s_iota, 1)
            pool.iota(iota_node[:, :, :], [[1, BL], [BL, P]], base=0, channel_multiplier=0,
                      allow_small_or_imprecise_dtypes=True).then_inc(s_iota, 1)

            pool.wait_ge(s_relu, 1)
            with pool.Fori(0, XRING) as lap:
                for k in range(XK):
                    pool.wait_ge(s_x[k], 16 * (lap + 1))
                    pool.sem_inc(s_held)
                    rows = xr[:, bass.ds(x_slot(lap, k), GW), :].rearrange("p w (b d) -> p (w b) d", d=D)
                    pool.tensor_tensor(rows, rows, brelu[:, None, :].to_broadcast([P, GW * BL, D]), ALU.add
                                       ).then_inc(s_early, 1)

            def gather_x(i, first):
                for g in range(RING):
                    n = i * RING + g
                    if not first:
                        pool.wait_ge(s_gather[g], 16 * LANES * i)
                    pool.tensor_copy(stage1[:, g, :], dst_list[:, bass.ds(n * LANES, LANES)]).then_inc(s_stage, 1)
                    pool.wait_ge(s_stage, n + 1)
                    for k in range(LANES):
                        if not first:
                            pool.wait_ge(s_T, n * LANES + k - TB + 1)
                            pool.sem_inc(s_held)
                        pool.indirect_dma_start(
                            xg[:, g * LANES + k, :], None, x,
                            bass.IndirectOffsetOnAxis(ap=stage1[:, g, k:k + 1], axis=0)).then_inc(s_gather[g], 16)

            pool.wait_ge(s_list, 1)
            gather_x(0, True)
            with pool.Fori(1, LAPS) as i:
                gather_x(i, False)

            def gather_message(stage, to, done):
                pool.indirect_dma_start(
                    to, None, msg, bass.IndirectOffsetOnAxis(ap=stage, axis=0),
                    bounds_check=ROWS - 1, oob_is_err=False).then_inc(done, 16)

            def gather_messages(lap, g, mend):
                if isinstance(lap, int) and lap == 0:
                    pool.wait_ge(s_lists, 1)
                else:
                    pool.wait_ge(s_lists, 1 + len(STAGED) * (lap - 1) + STAGED.index(f"w{g}") + 1 if mend else
                                 1 + len(STAGED) * FL + XK * (lap - 1 - FL) + g + 1)
                    pool.sem_inc(s_held)
                for k in range(GW):
                    gather_message(stage3[:, g, k:k + 1], gm[:, g * GW + k, :], s_wg[g * GW + k])

            def gather_fix(m, k):
                pool.wait_ge(s_lists, 1 + len(STAGED) * m + STAGED.index(f"f{k}") + 1)
                pool.sem_inc(s_held)
                gather_message(stage4[:, k, 0:1], fm[k], s_fg[k])
                pool.indirect_dma_start(
                    xf[k], None, x, bass.IndirectOffsetOnAxis(ap=stage4[:, k, 1:2], axis=0),
                    bounds_check=NODES - 1, oob_is_err=False).then_inc(s_fg[k], 16)

            def scatter_fix(m, k):
                pool.wait_ge(s_ff, m * FX + k + 1)
                pool.sem_inc(s_held)
                pool.indirect_dma_start(
                    out, bass.IndirectOffsetOnAxis(ap=stage4[:, k, 1:2], axis=0), xf[k], None,
                    bounds_check=NODES - 1, oob_is_err=False).then_inc(s_fs[k], 16)

            pool.wait_ge(s_win, 1)
            for g in range(RING):
                pool.wait_ge(s_mst[g], 16 * LAPS)
            pool.wait_ge(s_T, MT)
            for k in range(XK):
                pool.wait_ge(s_out[k], 16 * XRING)

            def gathers(lap, scatter, mend):
                for g in range(XK):
                    gather_messages(lap, g, mend)
                    if scatter:
                        scatter_fix(lap - 2, g)
                    if mend and g > 0:
                        gather_fix(lap - 1, g - 1)
                if mend:
                    gather_fix(lap - 1, XK - 1)

            gathers(0, False, False)
            gathers(1, False, True)
            with pool.Fori(2, FL + 1) as lap:
                gathers(lap, True, True)
            gathers(FL + 1, True, False)
            with pool.Fori(FL + 2, MAIN) as lap:
                gathers(lap, False, False)
            pool.wait_ge(s_wmm, (MAIN - 1) * WB + 1)
            gather_message(row_list[:, NW - 1:NW], gm[:, 0, :], s_wg[0])

        @block.scalar
        def _(act):
            act.dma_start(brelu[:, :], bias.rearrange("(a d) -> a d", a=1).to_broadcast([P, D])).then_inc(s_brelu, 16)
            act.wait_ge(s_brelu, 16)
            nc.scalar.activation(brelu[:, :], brelu[:, :], ACT.Relu).then_inc(s_relu, 1)

            def store_out(lap, k):
                if not (isinstance(lap, int) and lap == 0):
                    act.wait_ge(s_out[k], 16 * lap)
                act.dma_start(out_groups[bass.ds(lap * XK + k, 1)].rearrange("g p w n -> p (g w) n"),
                              xr[:, bass.ds(x_slot(lap, k), GW), :]).then_inc(s_out[k], 16)

            for k in range(XK):
                act.wait_ge(s_early, k + 1)
                store_out(0, k)
            LATE = (LANES - 1, LANES) + tuple(n * LANES - 1 for n in range(2, 6))
            for n in range(XK, XRING * XK - len(LATE)):
                act.wait_ge(s_early, n + 1)
                store_out(n // XK, n % XK)

            act.wait_ge(s_const, 1)
            nc.scalar.activation(sqrt_eps[:, :], eps[:, :], ACT.Sqrt)

            def deviations(i, g):
                act.wait_ge(s_var, (i * RING + g + 1) * LANES)
                nc.scalar.activation(std[:, g, :], mv[:, g, :, 1], ACT.Sqrt, bias=eps[:, 0:1]).then_inc(s_std, 1)

            def normalise(i, j, first):
                g, k = j // LANES, j % LANES
                if k == 0:
                    act.wait_ge(s_ln, i * RING + g + 1)
                nc.scalar.activation(xg[:, j, :], xg[:, j, :], ACT.Relu, bias=nmr[:, g, k:k + 1],
                                     scale=rstd[:, g, k:k + 1]).then_inc(s_norm, 1)

            def copy_hT(i, j, first):
                t = i * TB + j
                act.wait_ge(s_T, t + 1)
                if not (first and j < RING):
                    act.wait_ge(s_mm, t - RING + 1)
                nc.scalar.copy(hT[:, j % RING, :], ps_T[j % RING]).then_inc(s_hT, 1)

            def copy_messages(i, j, first):
                t = i * TB + j
                act.wait_ge(s_mm, t + 1)
                if not first and j % LANES == 0:
                    act.wait_ge(s_mst[j // LANES], 16 * i)
                nc.scalar.copy(mg[:, j, :], ps_M[j % RING]).then_inc(s_mg, 1)

            LAGS = ((3, normalise), (5, copy_hT), (7, copy_messages))

            def steps(i, first, second=False):
                for j in range(TB):
                    if j % LANES == LAGS[0][0] - 1:
                        deviations(i, j // LANES)
                    if (first or second) and i * TB + j in LATE:
                        n = XRING * XK - len(LATE) + LATE.index(i * TB + j)
                        act.wait_ge(s_early, n + 1)
                        store_out(n // XK, n % XK)
                    for lag, do in LAGS:
                        if j >= lag:
                            do(i, j - lag, first)
                        elif not first:
                            do(i - 1, j - lag + TB, second)

            steps(0, True)
            steps(1, False, True)
            with act.Fori(2, LAPS) as i:
                steps(i, False)
            for j in range(TB, TB + LAGS[-1][0]):
                for lag, do in LAGS:
                    if j - lag < TB:
                        do(LAPS - 1, j - lag, False)

            def stage_windows(lap, g):
                nc.scalar.copy(stage3[:, g, :], row_list[:, bass.ds(NE + lap * WB + g * GW, GW)]).then_inc(s_lists, 1)

            def stage_fix(m, k):
                if not (isinstance(m, int) and m == 0):
                    act.wait_ge(s_fs[k], 16 * m)
                    act.sem_inc(s_held)
                nc.scalar.copy(stage4[:, k, :], fix_list[:, bass.ds(m * FX + k, 1), :]
                               .rearrange("p w v -> p (w v)")).then_inc(s_lists, 1)

            def outputs(lap, windows_next, fix_next):
                for k in range(XK):
                    act.wait_ge(s_fin, lap * WB + (k + 1) * GW)
                    act.sem_inc(s_held)
                    store_out(lap + EL, k)
                    if windows_next:
                        stage_windows(lap + 1, k)
                    if fix_next and k > 0:
                        stage_fix(lap, k - 1)
                if fix_next:
                    stage_fix(lap, FX - 1)

            act.wait_ge(s_win, 1)
            nc.scalar.copy(stage3[:, :, :].rearrange("p g w -> p (g w)"), row_list[:, NE:NE + WB]).then_inc(s_lists, 1)
            outputs(0, True, True)
            with act.Fori(1, FL) as lap:
                outputs(lap, True, True)
            with act.Fori(FL, MAIN - 1) as lap:
                outputs(lap, True, False)
            outputs(MAIN - 1, False, False)
            act.wait_ge(s_fin, NW - NE)
            tail_dma(act, out, xt, False, s_outt)
            for k in range(XK):
                act.wait_ge(s_out[k], 16 * XLAPS)
            act.wait_ge(s_outt, 32)
            for k in range(FX):
                act.wait_ge(s_fs[k], 16 * FL)

            act.wait_ge(s_win, 1)
            n_over = act.value_load(over_i[0:1, 0:1], min_val=0, max_val=E)
            with act.If(n_over > 0):
                act.dma_start(xr[:, 0, :], x_wins[0]).then_inc(s_a_x, 16)
                with act.Fori(0, NW - 2) as w:
                    act.wait_ge(s_a_win, w + 2)
                    act.dma_start(out_wins[bass.ds(w, 1)].rearrange("w p n -> (w p) n"), xr[:, 0, :]
                                  ).then_inc(s_a_out, 16)
                    act.wait_ge(s_a_out, 16 * (w + 1))
                    act.dma_start(xr[:, 0, :], x_wins[bass.ds(w + 1, 1)].rearrange("w p n -> (w p) n")
                                  ).then_inc(s_a_x, 16)
                act.wait_ge(s_a_win, NW)
                act.dma_start(out_wins[NW - 2], xr[:, 0, :]).then_inc(s_a_out, 16)
                act.wait_ge(s_a_out, 16 * (NW - 1))
                tail_dma(act, x, xr[0:TAILP, 0, :], True, s_a_x)
                act.wait_ge(s_a_win, NW + 1)
                tail_dma(act, out, xr[0:TAILP, 0, :], False, s_a_out)
                act.wait_ge(s_a_out, 16 * (NW + 1))

        @block.tensor
        def _(pe):
            def mm(o, a, b, start=False, stop=False):
                return pe.matmul(o, a, b, start=start, stop=stop, skip_group_check=True)

            pe.wait_ge(s_tot, 1)
            tot = scan[0][:, :, PADC + EC - 1]
            mm(ps_rel, before16[0:EP, 0:EP], tot, True, True)
            mm(ps_cnt, ones16[0:EP, :], tot, True, True).then_inc(s_relps, 1)

            def scatter_dst(n, g, start):
                pe.wait_ge(s_sc, n + 1)
                for c in range(LANES):
                    last = mm(ps_dst, OHL[g][:, :, c], HV[g][:, :, c], start and c == 0)
                last.then_inc(s_scps, 1)

            for g in range(RING):
                scatter_dst(g, g, g == 0)
            with pe.Fori(1, LAPS) as i:
                for g in range(RING):
                    scatter_dst(i * RING + g, g, False)

            third = NG // RING

            def count_lanes(k):
                pe.wait_ge(s_ohw, k + 1)
                for n in range(k * third, (k + 1) * third):
                    for o, ws in ps_L:
                        last = mm(o, ident16[0:EP, 0:EP], OHW[:, n, ws, :], n == 0, n == NG - 1)
                if k == RING - 1:
                    last.then_inc(s_lt, 1)

            def first_ranks():
                pe.wait_ge(s_ohw, RING + 1)
                for o, ws in ps_L:
                    mm(o, before16[0:EP, 0:EP], LT[:, ws, :], True)
                    for l in range(LANES - 1):
                        to = LANES - 1 - l
                        last = mm(o[:, :, l + 1:LANES], ones16[0:EP, 0:EP],
                                  LT[:, ws, l:l + 1].to_broadcast([EP, ws.stop - ws.start, to]))
                last.then_inc(s_lt, 1)

            def transpose_tile(i, j, first):
                t = i * TB + j
                pe.wait_ge(s_norm, t + 1)
                if not (first and j < RING):
                    pe.wait_ge(s_hT, t - RING + 1)
                for k in range(KC):
                    last = pe.transpose(ps_T[j % RING][:, k * P:(k + 1) * P], xg[:, j, k * P:(k + 1) * P], ident[:, :])
                last.then_inc(s_T, 1)

            def multiply(i, j, first, rel):
                t = i * TB + j
                pe.wait_ge(s_hT, t + 1)
                if not (first and j < RING):
                    pe.wait_ge(s_mg, t - RING + 1)
                for k in range(KC):
                    last = mm(ps_M[j % RING], hT[:, j % RING, k * P:(k + 1) * P],
                              W[:, bass.ds(rel * (KC * D) + k * D, D)], k == 0, k == KC - 1)
                last.then_inc(s_mm, 1)

            def scatter_windows(n, g, start=False):
                pe.wait_ge(s_rv, n + 1)
                if start:
                    any_row = OHW[:, 0, 0:2 * NW // LANES + 1, :].rearrange("p w c -> p (w c)")[:, 0:2 * NW]
                    mm(ps_win, zeros16[0:EP, :], any_row, True)
                for c in range(LANES):
                    for v in range(2):
                        last = mm(ps_win[:, v * NW:(v + 1) * NW], RV[g][:, v, :, c],
                                  OHW[:, bass.ds(n, 1), :, c].rearrange("p n w -> p (n w)"))
                last.then_inc(s_rvps, 1)

            def load_rel(i, g):
                packed = pe.value_load(rel_i[0:1, bass.ds(i * RING + g, 1)], min_val=0, max_val=RB ** LANES - 1)
                return [(packed // RB ** k) % RB for k in range(LANES)]

            def body(i, first, second=False):
                rel = []
                for j in range(TB):
                    g = j // LANES
                    transpose_tile(i, j, first)
                    if j % LANES == 0:
                        rel += load_rel(i, g)
                    if j >= MLAG:
                        multiply(i, j - MLAG, first, rel[j])
                    elif not first:
                        multiply(i - 1, j - MLAG + TB, False, rel[j])
                    if j % LANES == LANES - 1:
                        if not first:
                            scatter_windows((i - 1) * RING + g, g, second and g == 0)

            pe.wait_ge(s_w, 16)
            pe.wait_ge(s_list, 1)
            for k in range(RING):
                count_lanes(k)
            first_ranks()
            body(0, True)
            body(1, False, True)
            with pe.Fori(2, LAPS) as i:
                body(i, False)
            rel = load_rel(LAPS, 0)
            for j in range(MLAG):
                multiply(LAPS - 1, TB - MLAG + j, False, rel[j])
            for g in range(RING):
                scatter_windows(NG - RING + g, g)
            pe.wait_ge(s_over, 1)
            mm(ps_over, ones16[0:EP, :], over16[:, :], True, True).then_inc(s_overps, 1)

            def sum_window(w, k, s, sel, rows, lap1):
                pw = ps_W[s]
                mm(pw[:, 0:2 * D], ones_b[:, :], bias3[:, :, :].rearrange("p a d -> p (a d)"), True)
                mm(pw[:, 2 * D:3 * D], ones_b[:, :], bias3[:, 0, :], True)
                pe.wait_ge(s_sel, w + 1)
                pe.wait_ge(s_wg[k], 16 * lap1)
                for b in range(BL):
                    last = mm(pw[:, b * D:(b + 1) * D], sel[:, b, :], rows)
                last.then_inc(s_wmm, 1)

            def fix_row(m, k, first):
                n = m * FX + k
                if not (first and k == 0):
                    pe.wait_ge(s_fq, n)
                pe.wait_ge(s_fd, n + 1)
                mm(ps_row, ones16[:, :], fd[k], True, True).then_inc(s_frow, 1)

            def fix_sum(m, k, first):
                n = m * FX + k
                if not (first and k < 2):
                    pe.wait_ge(s_ff, n - 1)
                mm(ps_fix[k], ones_b[:, :], bias3[:, 0, :], True)
                pe.wait_ge(s_fq, n + 1)
                pe.wait_ge(s_fg[k], 32 * (m + 1))
                mm(ps_fix[k], fq[k], fm[k]).then_inc(s_fsum, 1)

            def windows(lap, first, mend):
                for k in range(WB):
                    w = lap * WB + k
                    if not (first and k < 2):
                        pe.wait_ge(s_fin, w - 1)
                    sum_window(w, k, k % 2, S[:, k % SS], gm[:, k, :], lap + 1)
                    if mend:
                        (fix_row, fix_sum)[k % 2](lap - 1, k // 2, isinstance(lap, int) and lap == 1)

            pe.wait_ge(s_mg, MT)
            pe.wait_ge(s_bias3, 2)
            windows(0, True, False)
            windows(1, False, True)
            with pe.Fori(2, FL + 1) as lap:
                windows(lap, False, True)
            with pe.Fori(FL + 1, MAIN) as lap:
                windows(lap, False, False)
            pe.wait_ge(s_fin, NW - NE - 2)
            sum_window(NW - NE - 1, 0, 0, S[:, 0], gm[:, 0, :], MAIN + 1)

            pe.wait_ge(s_win, 1)
            n_over = pe.value_load(over_i[0:1, 0:1], min_val=0, max_val=E)
            with pe.If(n_over > 0):
                def scatter_src(c, start):
                    pe.wait_ge(s_a_sc, c + 1)
                    mm(ps_dst, a_lane, a_tile[:, :], start).then_inc(s_a_ps, 1)

                scatter_src(0, True)
                with pe.Fori(1, EC) as c:
                    scatter_src(c, False)
                with pe.Fori(0, NW) as w:
                    pe.wait_ge(s_a_win, w + 1)
                    mm(ps_W[0][:, 0:2 * D], ones_b[:, :], bias3[:, :, :].rearrange("p a d -> p (a d)"), True)
                    mm(ps_W[0][:, 2 * D:3 * D], ones_b[:, :], bias3[:, 0, :], True)
                    with pe.Fori(0, LAPS) as q:
                        pe.wait_ge(s_a_msg, 16 * (w * LAPS + q + 1))
                        for j in range(TB):
                            pe.wait_ge(s_a_sel, (w * LAPS + q) * TB + j + 1)
                            for b in range(BL):
                                last = mm(ps_W[0][:, b * D:(b + 1) * D], S[:, j % SS, b, :], xg[:, j, :])
                            last.then_inc(s_a_mm, 1)

        @block.vector
        def _(dve):
            v = nc.vector
            c = Count(dve, s_dve)

            def ts(o, a, s1, op0, s2=None, op1=None):
                if op1 is None:
                    return v.tensor_scalar(o, a, s1, None, op0)
                return v.tensor_scalar(o, a, s1, s2, op0, op1)

            def stt(o, a, s1, op0, b, op1):
                return v.scalar_tensor_tensor(out=o, in0=a, scalar=s1, in1=b, op0=op0, op1=op1)

            def tt(o, a, b, op):
                return v.tensor_tensor(o, a, b, op)

            def of_group(a, n, count):
                return a[:, bass.ds(n, 1), 0:LANES].to_broadcast([EP, count, LANES])

            def one_hot(o, a, n, count):
                return tt(o, iota_c[0:EP, 0:count, :], of_group(a, n, count), ALU.is_equal)

            def columns(a):
                return a[:, 0:EC // LANES, 0:LANES]

            def by_group(a):
                return a.rearrange("p (n c) -> p n c", c=LANES)

            v.memset(eps[:], EPS).then_inc(s_const, 1)
            for t, value in ((ones16, 1.0), (zeros16, 0.0), (ones_b, 1.0), (xt, 0.0), (tiles, 0.0), (rel_f, 0.0)):
                c.up(v.memset(t[:], value))
            c.up(v.memset(cols[:, 0:3, :, :], -1.0))
            c.up(v.memset(cols[:, 3:7, :, :], 0.0))
            for t in scan:
                c.up(v.memset(t[:, :, 0:PADC], 0.0))
            dve.wait_ge(s_iota, 3)
            c.up(v.tensor_copy(iota_c[:, :, :], iota16[:, :, None].to_broadcast([P, iota_n, LANES])))
            c.up(ts(ident[:, :], iota16[:, 0:P], part[:, 0:1], ALU.is_equal))
            c.up(ts(ident16[:, :], iota16[:, 0:P], part[:, 0:1], ALU.is_equal))
            done = c.up(ts(before16[:, :], iota16[:, 0:P], part[:, 0:1], ALU.is_gt))

            dve.wait_ge(s_edge, 48)
            c.wait(done)
            c.chain(v.tensor_copy(typ16[:, :], typ_i[:, :]))
            c.chain(tt(scan[2][:, :, PADC:], typ16[:, None, :].to_broadcast([EP, R, EC]),
                       iota16[0:EP, 0:R, None].to_broadcast([EP, R, EC]), ALU.is_equal))
            frm, to, step = scan[2], scan[0], 1
            while step < EC:
                assert step <= PADC
                ins = tt(to[:, :, PADC:], frm[:, :, PADC:], frm[:, :, PADC - step:PADC - step + EC], ALU.add)
                step *= 2
                if step >= EC:
                    ins.then_inc(s_tot, 1)
                    assert to is scan[0]
                else:
                    c.chain(ins)
                    frm, to = to, scan[1] if to is scan[0] else scan[0]

            dve.wait_ge(s_relps, 1)
            c.chain(ts(cnt_i[:, 0, :], ps_cnt, float(P - 1), ALU.add))
            c.chain(ts(cnt_i[:, 1, :], cnt_i[:, 0, :], P.bit_length() - 1, ALU.arith_shift_right))
            c.chain(v.tensor_copy(tiles[:, 0, R:], cnt_i[:, 1, :]))
            frm, to, step = 0, 1, 1
            while step < R:
                c.chain(tt(tiles[:, to, R:], tiles[:, frm, R:], tiles[:, frm, R - step:2 * R - step], ALU.add))
                frm, to, step = to, frm, 2 * step
            first_tile = tiles[:, frm, R - 1:2 * R - 1]
            c.chain(stt(base[:, :], first_tile[0:EP, :], float(P), ALU.mult, ps_rel, ALU.add))
            dve.wait_ge(s_tot, 1)
            c.chain(tt(sc_sum[:, :, :], scan[0][:, :, PADC:], base[:, :, None].to_broadcast([EP, R, EC]), ALU.add))
            c.chain(tt(sc_sel[:, :, :], sc_sum[:, :, :], scan[2][:, :, PADC:], ALU.mult))
            c.chain(v.tensor_reduce(pos[:, :], sc_sel[:, :, :].rearrange("p r c -> p c r"), AX_X, ALU.add))
            c.chain(ts(pos_i[:, :], pos[:, :], -1.0, ALU.add))
            c.up(ts(tmp_i[:, 0, :], pos_i[:, :], P - 1, ALU.bitwise_and))
            c.up(ts(tmp_i[:, 1, :], pos_i[:, :], P.bit_length() - 1, ALU.arith_shift_right))
            c.up(ts(tmp_i[:, 2, :], dst_i[:, :], 8, ALU.arith_shift_right))
            c.chain(ts(tmp_i[:, 3, :], dst_i[:, :], 255, ALU.bitwise_and))
            for k, t in enumerate((lane16, tile16, dhi16, dlo16)):
                done = c.up(v.tensor_copy(columns(t), by_group(tmp_i[:, k, :])))
            c.wait(done)

            def scatter_dst(i, g, first):
                n = i * RING + g
                if not first:
                    dve.wait_ge(s_scps, n - RING + 1)
                c.up(one_hot(OHL[g], lane16, n, P))
                c.chain(one_hot(OHT[g][:, 0:MT, :], tile16, n, MT))
                c.up(tt(HV[g][:, 0:MT, :], OHT[g][:, 0:MT, :], of_group(dhi16, n, MT), ALU.mult))
                tt(HV[g][:, MT:, :], OHT[g][:, 0:MT, :], of_group(dlo16, n, MT), ALU.mult).then_inc(s_sc, 1)

            for g in range(RING):
                scatter_dst(0, g, True)
            with dve.Fori(1, LAPS) as i:
                c.loop(i - 1, 3 * RING)
                for g in range(RING):
                    scatter_dst(i, g, False)
            c.end(LAPS - 1)

            c.chain(tt(rel_ge[:, :, :], iota16[0:1, 0:MT, None].to_broadcast([1, MT, R]),
                       first_tile[0:1, None, :].to_broadcast([1, MT, R]), ALU.is_ge))
            rel_of_tile = rel_f[:, MLAG:MLAG + MT]
            c.chain(v.tensor_reduce(rel_of_tile, rel_ge[:, :, :], AX_X, ALU.add))
            c.chain(ts(rel_of_tile, rel_of_tile, -1.0, ALU.add))
            digits = rel_f[:, :].rearrange("p (n k) -> p k n", k=LANES)
            acc = digits[:, LANES - 1, :]
            for k in reversed(range(1, LANES - 1)):
                c.chain(stt(rel_p[:, k, :], acc, float(RB), ALU.mult, digits[:, k, :], ALU.add))
                acc = rel_p[:, k, :]
            done = c.up(stt(rel_i[:, :], acc, float(RB), ALU.mult, digits[:, 0, :], ALU.add))
            dve.wait_ge(s_scps, NG)
            c.chain(v.tensor_copy(dlo_f[:, :], ps_dst[:, MT:2 * MT]))
            c.wait(done)
            stt(dst_list[:, :], ps_dst[:, 0:MT], 256.0, ALU.mult, dlo_f[:, :], ALU.add).then_inc(s_list, 1)

            c.chain(ts(tmp_i[:, 4, :], src_i[:, :], 7, ALU.arith_shift_right))
            c.chain(ts(tmp_i[:, 5, :], tmp_i[:, 4, :], float(DIV), ALU.mult))
            c.chain(ts(tmp_i[:, 6, :], tmp_i[:, 5, :], 9, ALU.arith_shift_right))
            c.chain(v.tensor_copy(columns(win16), by_group(tmp_i[:, 6, :])))
            third = NG // RING

            def window_hots(k):
                ws = slice(k * third, (k + 1) * third)
                tt(OHW[:, ws, :, :], iota_c[0:EP, None, 0:NW, :].to_broadcast([EP, third, NW, LANES]),
                   win16[:, ws, None, 0:LANES].to_broadcast([EP, third, NW, LANES]), ALU.is_equal).then_inc(s_ohw, 1)

            def group(i, g, tiles_too=True, columns_too=True, rv_used=True):
                n = i * RING + g
                m = n - RING
                if tiles_too:
                    dve.wait_ge(s_gather[g], 16 * LANES * (i + 1))
                    for k in range(LANES):
                        c.up(v.bn_stats(stats[:, g, k, :], xg[:, g * LANES + k, :]))
                if columns_too:
                    ohw = OHW[:, bass.ds(m, 1), :, :].rearrange("p n w c -> p (n w) c")
                    c.chain(tt(prod[:, :, :], ohw, C[:, :, :], ALU.mult))
                    with nc.allow_low_precision(reason="one term is not zero; whole numbers, exact up to 2048"):
                        rank = c.up(v.tensor_reduce(rank16[:, bass.ds(m, 1), 0:LANES].rearrange("p n c -> p (n c)"),
                                                    prod[:, :, :].rearrange("p w c -> p c w"), AX_X, ALU.add))
                else:
                    c.wait(c.base + c.n)
                if tiles_too:
                    for k in range(LANES):
                        v.bn_aggr(mv[:, g, k, :], stats[:, g, k, :]).then_inc(s_var, 1)
                if columns_too:
                    c.up(tt(C[:, :, :], C[:, :, :], ohw, ALU.add))
                    c.wait(rank)
                    if rv_used:
                        dve.wait_ge(s_rvps, m - RING + 1)
                    c.chain(one_hot(OHR[g], rank16, m, P))
                    c.up(tt(RV[g][:, 0, :, :], OHR[g], of_group(v1, m, P), ALU.mult))
                    tt(RV[g][:, 1, :, :], OHR[g], of_group(v2, m, P), ALU.mult).then_inc(s_rv, 1)
                if tiles_too:
                    dve.wait_ge(s_std, n + 1)
                    c.chain(v.reciprocal(rstd[:, g, :], std[:, g, :]))
                    stt(nmr[:, g, :], mv[:, g, :, 0], -1.0, ALU.mult, rstd[:, g, :], ALU.mult).then_inc(s_ln, 1)

            for k in range(RING):
                window_hots(k)
            group(0, 0, columns_too=False)
            dve.wait_ge(s_lt, 1)
            c.chain(v.tensor_copy(LT[:, ps_L[0][1], :], ps_L[0][0]))
            v.tensor_copy(LT[:, ps_L[1][1], :], ps_L[1][0]).then_inc(s_ohw, 1)
            dve.wait_ge(s_bias, 16)
            c.chain(v.tensor_copy(bias_part[:, 0, :], bias_row))
            c.chain(tt(bias_rest[:, 0, :], bias_row, bias_part[:, 0, :], ALU.subtract))
            c.chain(v.tensor_copy(bias_part[:, 1, :], bias_rest[:, 0, :]))
            c.chain(tt(bias_rest[:, 1, :], bias_rest[:, 0, :], bias_part[:, 1, :], ALU.subtract))
            c.chain(v.tensor_copy(bias_part[:, 2, :], bias_rest[:, 1, :]))
            group(0, 1, columns_too=False)
            c.chain(ts(bias_sel[:, 0, :], bias_part[:, 0, :], ident[0:3, 0:1], ALU.mult))
            c.chain(stt(bias_sel[:, 1, :], bias_part[:, 1, :], ident[0:3, 1:2], ALU.mult, bias_sel[:, 0, :],
                        ALU.add))
            for k in range(2):
                stt(bias3[:, k, :], bias_part[:, 2, :], ident[0:3, 2:3], ALU.mult, bias_sel[:, 1, :],
                    ALU.add).then_inc(s_bias3, 1)
            dve.wait_ge(s_lt, 2)
            for o, ws in ps_L:
                done = c.up(v.tensor_copy(C[:, ws, :], o))
            c.chain(stt(srel[:, :], tmp_i[:, 6, :], float(-WIN), ALU.mult, src_i[:, :], ALU.add))
            c.up(ts(tmp_i[:, 7, :], pos_i[:, :], 7, ALU.bitwise_and))
            c.chain(ts(tmp_i[:, 4, :], pos_i[:, :], 3, ALU.arith_shift_right))
            c.up(ts(columns(v1), by_group(tmp_i[:, 4, :]), 16.0, ALU.add))
            c.chain(stt(v2f[:, :], tmp_i[:, 7, :], 512.0, ALU.mult, srel[:, :], ALU.add))
            c.chain(ts(columns(v2), by_group(v2f[:, :]), -2048.0, ALU.add))
            group(0, 2, columns_too=False)
            for g in range(RING):
                group(1, g, rv_used=False)
            PER = RING * (LANES + 6)
            with dve.Fori(2, LAPS) as i:
                c.loop(i - 2, PER)
                for g in range(RING):
                    group(i, g)
            c.end(LAPS - 2)
            for g in range(RING):
                group(LAPS, g, tiles_too=False)

            c.chain(ts(over[:, :, 0:LANES], rank16[:, :, 0:LANES], float(P), ALU.is_ge))
            c.chain(v.tensor_reduce(over_n[:, :], over[:, :, 0:LANES], mybir.AxisListType.XY, ALU.add))
            v.tensor_copy(over16[:, :], over_n[:, :]).then_inc(s_over, 1)
            dve.wait_ge(s_overps, 1)
            c.up(v.tensor_copy(over_i[:, :], ps_over))
            dve.wait_ge(s_rvps, NG)
            empty, row = li_f[:, 6, :], li_f[:, 1, :]
            c.chain(v.tensor_copy(li[:, 0, :], ps_win[:, 0:NW]))
            c.up(ts(li[:, 1, :], ps_win[:, NW:2 * NW], 2048.0, ALU.add))
            c.chain(ts(empty, ps_win[:, 0:NW], 0.5, ALU.is_lt))
            c.up(ts(li[:, 2, :], li[:, 0, :], 4, ALU.arith_shift_right))
            c.up(ts(li[:, 3, :], li[:, 0, :], 15, ALU.bitwise_and))
            c.up(ts(li[:, 4, :], li[:, 1, :], 9, ALU.arith_shift_right))
            c.chain(ts(li[:, 5, :], li[:, 1, :], 511, ALU.bitwise_and))
            c.up(stt(src_list[:, :], empty, -1024.0, ALU.mult, li[:, 5, :], ALU.add))
            c.chain(stt(row, li[:, 3, :], 8.0, ALU.mult, li[:, 4, :], ALU.add))
            c.chain(stt(row, row, float(MT), ALU.mult, li[:, 2, :], ALU.add))
            c.chain(ts(row, row, -1.0, ALU.add))
            node = li_f[:, 2, 0:NE]
            c.up(stt(fix_list[:, :, 0], empty[:, 0:NE], float(NONE), ALU.mult, row[:, 0:NE], ALU.add))
            c.chain(stt(node, iota16[:, 0:NE], float(WIN), ALU.mult, li[:, 5, 0:NE], ALU.add))
            c.chain(stt(fix_list[:, :, 1], empty[:, 0:NE], float(NONE), ALU.mult, node, ALU.add))
            stt(row_list[:, :], empty, float(NONE), ALU.mult, row, ALU.add).then_inc(s_win, 1)
            dve.wait_ge(s_win, 1)

            def select(lap, k, first):
                w = lap * WB + k
                if not (first and k < SS):
                    dve.wait_ge(s_wmm, w - SS + 1)
                ts(S[:, k % SS], iota_node[:, :, :], src_list[:, bass.ds(w + NE, 1)], ALU.is_equal).then_inc(s_sel, 1)

            def finish(lap, k):
                w = lap * WB + k
                dve.wait_ge(s_wmm, w + 1)
                if k % GW == 0:
                    dve.wait_ge(s_x[k // GW], 16 * (lap + XRING + 1))
                xs = xr[:, bass.ds(x_slot(lap + XRING, 0) + k, 1), :].rearrange("p w n -> p (w n)")
                stt(xs, ps_W[k % 2], 0.0, ALU.max, xs, ALU.add).then_inc(s_fin, 1)

            def fix_src(m, k):
                ts(fd[k], ident16[:, :], src_list[:, bass.ds(m * FX + k, 1)], ALU.mult).then_inc(s_fd, 1)

            def fix_equal(m, k):
                dve.wait_ge(s_frow, m * FX + k + 1)
                ts(fq[k], ps_row, src_list[:, bass.ds(m * FX + k, 1)], ALU.is_equal).then_inc(s_fq, 1)

            def fix_finish(m, k):
                dve.wait_ge(s_fsum, m * FX + k + 1)
                dve.wait_ge(s_fg[k], 32 * (m + 1))
                stt(xf[k], ps_fix[k], 0.0, ALU.max, xf[k], ALU.add).then_inc(s_ff, 1)

            def windows(lap, first, mend, last=False):
                for k in range(WB):
                    if mend and k % 2 == 0:
                        fix_src(lap - 1, k // 2)
                    finish(lap, k)
                    if mend and k % 2 == 0 and k > 0:
                        fix_finish(lap - 1, k // 2 - 1)
                    if k + 2 < WB:
                        select(lap, k + 2, first)
                    elif k + 2 == WB or not last:
                        select(lap + 1, k + 2 - WB, False)
                    if mend and k % 2 == 0:
                        fix_equal(lap - 1, k // 2)
                if mend:
                    fix_finish(lap - 1, FX - 1)

            for k in range(2):
                select(0, k, True)
            for g in range(RING):
                dve.wait_ge(s_mst[g], 16 * LAPS)
            windows(0, True, False)
            windows(1, False, True)
            with dve.Fori(2, FL + 1) as lap:
                windows(lap, False, True)
            with dve.Fori(FL + 1, MAIN - 1) as lap:
                windows(lap, False, False)
            windows(MAIN - 1, False, False, True)
            dve.wait_ge(s_wmm, NW - NE)
            dve.wait_ge(s_tail, 32)
            stt(xt[:, :], ps_W[0][0:TAILP, :], 0.0, ALU.max, xt[:, :], ALU.add).then_inc(s_fin, 1)

            n_over = dve.value_load(over_i[0:1, 0:1], min_val=0, max_val=E)
            with dve.If(n_over > 0):
                dve.wait_ge(s_fin, NW - NE)
                for k in range(FX):
                    dve.wait_ge(s_fs[k], 16 * FL)
                c.up(ts(tmp_i[:, 0, :], src_i[:, :], 8, ALU.arith_shift_right))
                c.chain(ts(tmp_i[:, 1, :], src_i[:, :], 255, ALU.bitwise_and))
                c.up(ts(a_val[:, 0, :], tmp_i[:, 0, :], 1.0, ALU.add))
                c.chain(v.tensor_copy(a_val[:, 1, :], tmp_i[:, 1, :]))
                c.up(v.tensor_copy(by_group(a_pos[:, 0, :]), columns(lane16)))
                c.chain(v.tensor_copy(by_group(a_pos[:, 1, :]), columns(tile16)))

                def scatter_src(col, first):
                    one = bass.ds(col, 1)
                    if not first:
                        dve.wait_ge(s_a_ps, col)
                    c.up(ts(a_lane, iota16[0:EP, 0:P], a_pos[:, 0, one], ALU.is_equal))
                    c.chain(ts(a_tile[:, 0:MT], iota16[0:EP, 0:MT], a_pos[:, 1, one], ALU.is_equal,
                               a_val[:, 0, one], ALU.mult))
                    ts(a_tile[:, MT:2 * MT], iota16[0:EP, 0:MT], a_pos[:, 1, one], ALU.is_equal,
                       a_val[:, 1, one], ALU.mult).then_inc(s_a_sc, 1)

                scatter_src(0, True)
                with dve.Fori(1, EC) as col:
                    c.loop(col - 1, 2)
                    scatter_src(col, False)
                c.end(EC - 1)
                dve.wait_ge(s_a_ps, EC)
                c.chain(ts(dlo_f[:, :], ps_dst[:, MT:2 * MT], -256.0, ALU.add))
                c.chain(stt(src_slot[:, :], ps_dst[:, 0:MT], 256.0, ALU.mult, dlo_f[:, :], ALU.add))
                v.memset(over[:, 0, :], 0.0).then_inc(s_a_mm, SS)
                v.memset(over16[:, :], 0.0).then_inc(s_a_win, 1)

                def window(w, parts, done_x):
                    with dve.Fori(0, LAPS) as q:
                        for j in range(TB):
                            dve.wait_ge(s_a_mm, (w * LAPS + q) * TB + j + 1)
                            ts(S[:, j % SS], iota_node[:, :, :], src_slot[:, bass.ds(q * TB + j, 1)],
                               ALU.is_equal).then_inc(s_a_sel, 1)
                    dve.wait_ge(s_a_mm, SS + (w + 1) * MT)
                    c.chain(ts(src_slot[:, :], src_slot[:, :], float(-WIN), ALU.add))
                    dve.wait_ge(s_a_x, done_x)
                    stt(xr[0:parts, 0, :], ps_W[0][0:parts, :], 0.0, ALU.max, xr[0:parts, 0, :],
                        ALU.add).then_inc(s_a_win, 1)

                with dve.Fori(0, NW - 1) as w:
                    c.loop(w, 1)
                    window(w, P, 16 * (w + 1))
                c.end(NW - 1)
                window(NW - 1, TAILP, 16 * (NW + 1))


_INS = ["x", "src", "dst", "edge_type_8", "L0_gnn_weight", "L0_gnn_bias"]


def kernel(**inputs):
    import numpy as _np
    import concourse.bacc as _bacc
    from concourse import mybir as _mybir
    from concourse.bass_utils import run_bass_kernel_spmd as _run

    nc = _bacc.Bacc("TRN2", target_bir_lowering=False, num_devices=1)
    arrays, args = {}, []
    for name in _INS:
        a = _np.ascontiguousarray(inputs[name])
        arrays[f"in_{name}"] = a
        args.append(nc.dram_tensor(f"in_{name}", a.shape, _mybir.dt.from_np(a.dtype), kind="ExternalInput").ap())
    shape = arrays["in_x"].shape
    args.append(nc.dram_tensor("out_0", shape, _mybir.dt.float32, kind="ExternalOutput").ap())
    gnn_kernel(nc, *args)
    r = _run(nc, [arrays], core_ids=[0])
    return r.results[0]["out_0"]
```
